# Optimizing a Trainium2 kernel written in Bass

```python
import numpy as np
import jax
import jax.numpy as jnp

def _softmax(x, axis=-1):
    return jax.nn.softmax(x, axis=axis)

def _gelu(x):
    return jax.nn.gelu(x, approximate=True)

def _silu(x):
    return jax.nn.silu(x)

def _sigmoid(x):
    return jax.nn.sigmoid(x)

def _layernorm(x, axis=-1, eps=1e-05):
    m = jnp.mean(x, axis=axis, keepdims=True)
    v = jnp.var(x, axis=axis, keepdims=True)
    return (x - m) / jnp.sqrt(v + eps)

def _scatter_add(tgt, idx, src, axis=0):
    return tgt.at[idx].add(src)

def _segment_sum(src, seg, n):
    return jax.ops.segment_sum(src, seg, n)
kernel_name = 'mk_adj_resnorm_d2_adj_r2_647bff'

def setup_inputs(seed: int=0):
    np.random.seed(seed)
    _w = jnp.asarray

    def _rec_inputs():
        import jax
        import jax.numpy as jnp
        _gk = jax.random.key(seed)
        x = -0.0002928 + 1 * jax.random.normal(jax.random.fold_in(_gk, 1), (2048, 512), jnp.float32)
        _w = (1.0 + jnp.arange(2048, dtype=jnp.float32)) ** (-0.5)
        _w = _w / _w.mean()
        _pij = jnp.clip(0.0078125 * _w[:, None] * _w[None, :], 0.0, 1.0)
        _a = jax.random.uniform(jax.random.fold_in(_gk, 2), (2048, 2048)) < _pij
        _af = _a.astype(jnp.float32)
        adj = _af
        return (x, adj)
    x, adj = _rec_inputs()

    def _L0_gnn_setup():
        import jax, jax.numpy as jnp
        import numpy as np
        N = 2048
        D_IN = 512
        H = 16
        DH = D_IN // H
        ALPHA = 0.2
        MASK_VAL = -65500.0
        key = jax.random.key(seed)
        ks = jax.random.split(key, 7)
        x = jax.random.normal(ks[0], (N, D_IN), dtype=jnp.float32)
        adj = jax.random.randint(ks[1], (N, N), 0, 2).astype(jnp.float32)
        s = 1.0 / np.sqrt(D_IN)
        W_seq = jax.random.normal(ks[2], (D_IN, D_IN), dtype=jnp.float32) * s
        a1 = jax.random.normal(ks[3], (DH,), dtype=jnp.float32) / np.sqrt(DH)
        a2 = jax.random.normal(ks[4], (DH,), dtype=jnp.float32) / np.sqrt(DH)
        W_out = jax.random.normal(ks[5], (D_IN, D_IN), dtype=jnp.float32) * s
        b_out = jax.random.normal(ks[6], (D_IN,), dtype=jnp.float32) * 0.01
        return {'x': x, 'adj': adj, 'W_seq': W_seq, 'a1': a1, 'a2': a2, 'W_out': W_out, 'b_out': b_out}
    _L0_gnn_all = _L0_gnn_setup()
    _L0_gnn_in = {k: v for k, v in _L0_gnn_all.items() if k in ('W_seq', 'a1', 'a2', 'W_out', 'b_out')}
    del _L0_gnn_all

    def _L1_gnn_setup():
        import jax, jax.numpy as jnp
        import numpy as np
        N = 4096
        D = 512

        def adjacent_mat(adj):
            adj = adj + jnp.eye(adj.shape[0], dtype=adj.dtype)
            deg = jnp.sum(adj, axis=1)
            dinv = jnp.where(deg > 0, deg ** (-0.5), 0.0).astype(adj.dtype)
            return dinv[:, None] * adj * dinv[None, :]
        key = jax.random.key(seed)
        k1, k2 = jax.random.split(key)
        x = jax.random.normal(k1, (N, D), dtype=jnp.float32)
        Coefficient2 = 1e-08 * jnp.ones((N, N), dtype=jnp.float32)
        A = jax.random.uniform(k2, (N, N), dtype=jnp.float32)
        return {'x': x, 'Coefficient2': Coefficient2, 'A': A}
    _L1_gnn_all = _L1_gnn_setup()
    _L1_gnn_in = {k: v for k, v in _L1_gnn_all.items() if k in ()}
    del _L1_gnn_all
    return {'x': x, 'adj': adj, 'L0_gnn_W_seq': _L0_gnn_in['W_seq'], 'L0_gnn_a1': _L0_gnn_in['a1'], 'L0_gnn_a2': _L0_gnn_in['a2'], 'L0_gnn_W_out': _L0_gnn_in['W_out'], 'L0_gnn_b_out': _L0_gnn_in['b_out']}

def reference(x, adj, L0_gnn_W_seq, L0_gnn_a1, L0_gnn_a2, L0_gnn_W_out, L0_gnn_b_out):
    import jax
    import jax.numpy as jnp

    def _L0_gnn_ref(x, adj, W_seq, a1, a2, W_out, b_out):
        import jax, jax.numpy as jnp
        import numpy as np
        N = 2048
        D_IN = 512
        H = 16
        DH = D_IN // H
        ALPHA = 0.2
        MASK_VAL = -65500.0
        seq = (x @ W_seq).reshape(N, H, DH)
        score1 = jnp.einsum('nhd,d->hn', seq, a1)
        score2 = jnp.einsum('nhd,d->hn', seq, a2)
        scores = score1[:, :, None] + score2[:, None, :]
        scores = jax.nn.leaky_relu(scores, negative_slope=ALPHA)
        scores = scores + (1.0 - adj)[None, :, :] * MASK_VAL
        attn = jax.nn.softmax(scores, axis=-1)
        hidden = jnp.einsum('hij,jhd->ihd', attn, seq).reshape(N, D_IN)
        hidden = hidden @ W_out + b_out
        return jax.nn.elu(hidden)

    def _L1_gnn_ref(x, Coefficient2, A):
        import jax, jax.numpy as jnp
        import numpy as np
        N = 4096
        D = 512

        def adjacent_mat(adj):
            adj = adj + jnp.eye(adj.shape[0], dtype=adj.dtype)
            deg = jnp.sum(adj, axis=1)
            dinv = jnp.where(deg > 0, deg ** (-0.5), 0.0).astype(adj.dtype)
            return dinv[:, None] * adj * dinv[None, :]
        A_c = jax.lax.stop_gradient(A)
        adj = adjacent_mat((A_c + A_c.T) * 0.5)
        y = Coefficient2 @ adj
        y = y @ x
        return y
    x = _layernorm(x + _L0_gnn_ref(x, adj, L0_gnn_W_seq, L0_gnn_a1, L0_gnn_a2, L0_gnn_W_out, L0_gnn_b_out), axis=-1)
    x = _layernorm(x + _L1_gnn_ref(x, adj, adj), axis=-1)
    return x

_drawn_inputs = setup_inputs


def setup_inputs(seed=0):
    import zlib

    import numpy as np

    out = dict(_drawn_inputs(seed))
    spreads = {}
    factors = {}
    for name, (base, spread) in spreads.items():
        noise = np.random.default_rng([zlib.crc32(name.encode()), seed]).standard_normal(out[name].shape)
        drawn = base * np.exp(spread * noise) if base else spread * noise
        out[name] = jnp.asarray(drawn.astype(out[name].dtype))
    for name, factor in factors.items():
        out[name] = (out[name] * factor).astype(out[name].dtype)
    return out
```

```python
import numpy as np
import concourse.bass as bass
from concourse import mybir
from contextlib import ExitStack


def gat_then_normalised_adjacency(nc, x, adj, w_seq, a1, a2, w_out, b_out, out, s1_rows, nonempty_row):
    f32, bf16, f16 = mybir.dt.float32, mybir.dt.bfloat16, mybir.dt.float16
    ALU, ACT, AX = mybir.AluOpType, mybir.ActivationFunctionType, mybir.AxisListType

    P = 128
    N, D = x.shape
    NT = N // P
    H = 16
    DH = D // H
    DV = DH + 1
    KC = D // P
    SLOPE = 0.2
    EPS = 1e-5
    BIG = 2.0 ** 60
    SPLIT = 2.0 ** 11
    UNSPLIT = 1.0 / SPLIT
    TOP = 2.0 ** 14
    XS = 2.0 ** 9
    ZS = 2.0 ** 4
    NG = 8
    NZ = 4
    DIRECT = (3, 7, 11, 15)
    NV = NT - len(DIRECT)
    IB = 3
    NB = -(-NT // IB)
    HALF = NT // 2
    ACTZ = [j for j in range(NT) if j not in DIRECT]
    AT_SUMS, AT_HIGH, AT_LOW, AT_HID = 5, 8, 10, 13
    assert (2 * NV) % NZ == 0 and (2 * NT) % NG == 0

    ctx = ExitStack()
    with ctx:
        def sb(name, shape, dt):
            return ctx.enter_context(nc.sbuf_tensor(name, shape, dt))

        def sem(name):
            return ctx.enter_context(nc.semaphore(name))

        MT = sb("MT", [P, NT, N], bf16)
        SEQ = sb("SEQ", [P, NT, H, DV], f32)
        X1 = SEQ[:, :, :, :].rearrange("p t h d -> p t (h d)")
        RG = sb("RG", [P, 8192], f32)
        adj_f = RG[:, 0:2 * N].rearrange("p (u n) -> p u n", u=2)
        G = RG[:, :].bitcast(bf16).rearrange("p (s n) -> p s n", s=NG)
        XH = RG[:, :].bitcast(f16).rearrange("p (l t d) -> p l t d", l=2, t=NT)
        RZ = sb("RZ", [P, 8192], f32)
        ZH = RZ[:, :].bitcast(f16).rearrange("p (l t d) -> p l t d", l=2, t=NT)
        Z = RZ[:, 0:4096].bitcast(bf16).rearrange("p (s n) -> p s n", s=NZ)
        S1B = RZ[:, 4096:8192].rearrange("p (u n) -> p u n", u=2)
        adj_b = RZ[:, 0:2048].bitcast(bf16).rearrange("p (u n) -> p u n", u=2)
        mask_b = RZ[:, 2048:4096].bitcast(bf16).rearrange("p (u n) -> p u n", u=2)
        WS = RZ[:, 4096:6144].rearrange("p (k d) -> p k d", k=KC)
        xs = RZ[:, 6144:7168].rearrange("p (u d) -> p u d", u=2)
        xT = RZ[:, 7168:8192].rearrange("p (u d) -> p u d", u=2)
        WO = RZ[:, 4096:6144].rearrange("p (k d) -> p k d", k=KC)
        wk = RZ[:, 0:4096].rearrange("p (b u d) -> p b u d", b=4, u=2)
        hT, xr, vv, ee = wk[:, 0], wk[:, 1], wk[:, 2], wk[:, 3]
        wk2 = RZ[:, 6144:8192].rearrange("p (b u d) -> p b u d", b=2, u=2)
        rr, v2x = wk2[:, 0], wk2[:, 1]
        PNB = 2 * NT * 6 * DV
        RP = sb("RP", [P, 3 * NT * P], f32)
        assert PNB // 2 + NT * 5 * DV <= 3 * NT * P
        PN = RP[:, 0:PNB // 2].bitcast(f16).rearrange("p (u t c d) -> p u t c d", u=2, t=NT, c=6)
        o = PNB // 2
        T = RP[:, o:o + NT * 2 * DV].rearrange("p (t e d) -> p t e d", t=NT, e=2)
        o += NT * 2 * DV
        V2 = RP[:, o:o + NT * 2 * DV].rearrange("p (t e d) -> p t e d", t=NT, e=2)
        o += NT * 2 * DV
        ND = RP[:, o:o + NT * DV].rearrange("p (t d) -> p t d", t=NT)
        APN = RP[:, 0:2 * NT * P].rearrange("p (u t i) -> p u t i", u=2, t=NT)
        S2P = RP[:, 2 * NT * P:3 * NT * P].bitcast(bf16).rearrange("p (u t i) -> p u t i", u=2, t=NT)
        W5 = sb("W5", [P, 4, D], f32)
        WAtmp = W5[:, :, :].rearrange("p k (h d) -> p (k h) d", d=DH)
        BB = W5[:, 0, :]
        HC = W5[:, 2:4, :]
        s1T = W5[0:H, :, :].rearrange("p k d -> p (k d)")
        lw, yw = W5[:, 0:2, :], W5[:, 2:4, :]
        idf = sb("idf", [P, P], f32)
        idb = sb("idb", [P, P], bf16)
        id2 = sb("id2", [P, P], bf16)
        mone = sb("mone", [P, 1], f32)
        ones = sb("ones", [P, NT], bf16)
        NEB = sb("NEB", [P, N], bf16)
        TAB = sb("TAB", [P, 6, H, NT], f32)
        S1, S2, EE, FF, AA, BBT = (TAB[:, i] for i in range(6))
        VMT = T[:, :, 0, 0:H]
        VM = sb("VM", [P, H], f32)
        C2 = sb("C2", [P, H], f32)
        RV = sb("RV", [P, H], f32)
        red = sb("red", [P, 2, H], f32)
        KB = sb("KB", [P, 2, NT], f32)
        RS = sb("RS", [P, 2], f32)
        ROW = sb("ROW", [P, NT], f32)
        EMP = sb("EMP", [P, NT], f32)
        DINV = sb("DINV", [P, NT], f32)
        DSX = sb("DSX", [P, NT], f32)
        DSZ = sb("DSZ", [P, NT], f32)
        DSL = sb("DSL", [P, NT], f32)
        NEr = sb("NEr", [NT, P], bf16)
        RD = sb("RD", [P, NT], f32)
        AV = sb("AV", [P, 2, DH], f32)
        WA = sb("WA", [P, KC, 2 * H], f32)
        bst = sb("bst", [P, 2, 6], f32)
        mv = sb("mv", [P, 2, 2], f32)
        vps = sb("vps", [P, 2], f32)
        rstd = sb("rstd", [P, 2], f32)
        mhalf = sb("mhalf", [P, NT], f32)

        RMAX = bass.bass_isa.ReduceOp.max
        pb = [ctx.enter_context(nc.psum_tensor(f"bank{i}", [P, 512], f32)) for i in range(8)]

        consts = sem("consts")
        wseq_in = sem("wseq_in")
        a_in = sem("a_in")
        x_in = [sem(f"x_in{u}") for u in range(2)]
        adj_in = [sem(f"adj_in{u}") for u in range(2)]
        xT_ps = sem("xT_ps")
        xT_sb = sem("xT_sb")
        wa_done = sem("wa_done")
        seq_ps = sem("seq_ps")
        s_ps = sem("s_ps")
        seq_sb = sem("seq_sb")
        s_sb = sem("s_sb")
        adjb_done = sem("adjb_done")
        mask_done = sem("mask_done")
        col_ps = sem("col_ps")
        mtA_ps = sem("mtA_ps")
        mtB_ps = sem("mtB_ps")
        mtA_sb = sem("mtA_sb")
        mtB_sb = sem("mtB_sb")
        dve = sem("dve_step")
        pool = sem("pool_step")
        act = sem("act_step")
        vm_done = sem("vm_done")
        red_done = sem("red_done")
        allred = sem("allred")
        s1T_ps = sem("s1T_ps")
        s1T_sb = sem("s1T_sb")
        s1_stored = sem("s1_stored")
        texp_in = sem("texp_in")
        texp_out = sem("texp_out")
        tabs_done = sem("tabs_done")
        ne_sb = sem("ne_sb")
        ne_stored = sem("ne_stored")
        ne_in = sem("ne_in")
        ne_ps = sem("ne_ps")
        s1b_in = [sem(f"s1b_in{u}") for u in range(2)]
        kb_ready = sem("kb_ready")
        v2_ready = sem("v2_ready")
        hi_ready = sem("hi_ready")
        pn_ready = sem("pn_ready")
        z_ready = sem("z_ready")
        g_ready = sem("g_ready")
        g_used = sem("g_used")
        lo_out = sem("lo_out")
        bank_free = sem("bank_free")
        comb_ready = sem("comb_ready")
        hid_done = sem("hid_done")
        hc_done = sem("hc_done")
        deg_done = sem("deg_done")
        pow_done = sem("pow_done")
        row_done = sem("row_done")
        dscale = sem("dscale")
        wout_in = sem("wout_in")
        bb_in = sem("bb_in")
        xr_in = [sem(f"xr_in{u}") for u in range(2)]
        hT_ps = sem("hT_ps")
        hT_sb = sem("hT_sb")
        o_ps = sem("o_ps")
        xm_done = sem("xm_done")
        v_added = sem("v_added")
        ex_done = sem("ex_done")
        var_done = sem("var_done")
        rstd_done = sem("rstd_done")
        v2x_done = sem("v2x_done")
        xh_done = sem("xh_done")
        xl_done = sem("xl_done")
        ap_in = [sem(f"ap_in{u}") for u in range(2)]
        s2_done = sem("s2_done")
        y_ps = sem("y_ps")
        yl_done = sem("yl_done")
        yv_done = sem("yv_done")
        zh_done = sem("zh_done")
        zl_done = sem("zl_done")
        pan_done = sem("pan_done")
        o2_ps = sem("o2_ps")
        ol_done = sem("ol_done")
        var2_done = sem("var2_done")
        rstd2_done = sem("rstd2_done")
        ov_done = sem("ov_done")
        out_ready = sem("out_ready")
        out_st = [sem(f"out_st{u}") for u in range(2)]

        class Steps:

            def __init__(self, s):
                self.s, self.n, self.made = s, 0, 0

            def mark(self, ins):
                ins.then_inc(self.s, 1)
                self.n = self.n + 1
                self.made = self.made + 1

            def wait(self, eng):
                eng.wait_ge(self.s, self.n)

            def enter(self, i, start, per):
                self.base, self.start, self.per, self.made = self.n, start, per, 0
                self.n = i * per + (self.base - start * per)

            def leave(self, end):
                assert self.made == self.per
                self.n = self.base + (end - self.start) * self.per

        block = ctx.enter_context(nc.Block())
        DS = bass.ds

        def sums(b, n):
            return pb[b][:, 0:n * 4 * DV].rearrange("p (i e l d) -> p i e l d", i=n, e=2, l=2)

        @block.sync
        def _(sp):
            sp.dma_start(WS, w_seq.rearrange("(k p) d -> p k d", p=P)).then_inc(wseq_in, 16)
            for i, a in enumerate((a1, a2)):
                sp.dma_start(AV[:, i, :], a.rearrange("(o d) -> o d", o=1).broadcast_to([P, DH])).then_inc(a_in, 16)

            def load_x(t, u):
                sp.dma_start(xs[:, u, :], x[DS(t * P, P), :]).then_inc(x_in[u], 16)

            def load_adj(t, u):
                sp.dma_start(adj_f[:, u, :], adj[DS(t * P, P), :]).then_inc(adj_in[u], 16)

            for u in range(2):
                load_x(u, u)
                load_adj(u, u)
            with sp.Fori(1, NT // 2) as p:
                for u in range(2):
                    t = p * 2 + u
                    sp.wait_ge(xT_ps, t - 1)
                    load_x(t, u)
                    sp.wait_ge(adjb_done, t - 1)
                    load_adj(t, u)
            sp.wait_ge(s1T_sb, KC)
            sp.dma_start(s1_rows[:, :], s1T).then_inc(s1_stored, 16)
            sp.wait_ge(ne_sb, 1)
            sp.dma_start(nonempty_row.rearrange("(t p) -> t p", p=P), NEr[:, :]).then_inc(ne_stored, 16)
            sp.wait_ge(s1_stored, 16)

            def load_s1(h, u):
                sp.dma_start(S1B[:, u, :], s1_rows[DS(h, 1), :].broadcast_to([P, N])).then_inc(s1b_in[u], 16)

            sp.wait_ge(s_ps, NT)
            load_s1(0, 0)
            load_s1(1, 1)
            sp.wait_ge(ne_stored, 16)
            sp.dma_start(NEB[:, :], nonempty_row.rearrange("(o n) -> o n", o=1).broadcast_to([P, N])).then_inc(ne_in, 16)
            with sp.Fori(1, H // 2) as p:
                for u in range(2):
                    h = p * 2 + u
                    sp.wait_ge(z_ready, h * NV - NV)
                    sp.wait_ge(g_ready, h * NT - NT)
                    load_s1(h, u)
            sp.wait_ge(z_ready, (H - 1) * NV)
            sp.wait_ge(g_ready, (H - 1) * NT)
            sp.dma_start(WO, w_out.rearrange("(k p) d -> p k d", p=P)).then_inc(wout_in, 16)
            sp.dma_start(BB, b_out.rearrange("(o d) -> o d", o=1).broadcast_to([P, D])).then_inc(bb_in, 16)

            def load_xr(t, u):
                sp.dma_start(xr[:, u, :], x[DS(t * P, P), :]).then_inc(xr_in[u], 16)

            def load_ap(t, u):
                sp.dma_start(APN[:, u, :, :],
                             adj.rearrange("(t p) i -> p t i", p=P)[:, :, DS(t * P, P)]).then_inc(ap_in[u], 16)

            sp.wait_ge(g_ready, H * NT)
            for u in range(2):
                load_xr(u, u)
            sp.wait_ge(g_used, H * NT + NG)
            sp.wait_ge(hid_done, H)
            for u in range(2):
                load_ap(u, u)
            with sp.Fori(1, NT // 2) as p:
                for u in range(2):
                    t = p * 2 + u
                    sp.wait_ge(var_done, t - 1)
                    load_xr(t, u)
            with sp.Fori(1, NT // 2) as p:
                for u in range(2):
                    t = p * 2 + u
                    sp.wait_ge(s2_done, t - 1)
                    load_ap(t, u)
            with sp.Fori(0, NT // 2) as p:
                for u in range(2):
                    t = p * 2 + u
                    sp.wait_ge(out_ready, t + 1)
                    sp.dma_start(out[DS(t * P, P), :], yw[:, u, :]).then_inc(out_st[u], 16)
            for u in range(2):
                sp.wait_ge(out_st[u], 16 * (NT // 2))

        @block.gpsimd
        def _(gp):
            own = Steps(pool)
            own.mark(gp.memset(idf[:, :], 0.0))
            own.mark(gp.memset(idb[:, :], 0.0))
            own.mark(gp.memset(id2[:, :], 0.0))
            own.mark(gp.memset(mone[:, :], -1.0))
            gp.memset(ones[:, :], 1.0).then_inc(consts, 1)
            gp.memset(MT[:, 0, 0:P], 0.0).then_inc(consts, 1)
            gp.memset(mhalf[:, :], -0.5).then_inc(consts, 1)
            own.wait(gp)
            for m, one in ((idf, 1.0), (idb, 1.0), (id2, 2.0)):
                gp.affine_select(out=m[:, :], in_=m[:, :], compare_op=ALU.not_equal, fill=one, base=0,
                                 pattern=[[-1, P]], channel_multiplier=1).then_inc(consts, 1)
            gp.wait_ge(red_done, 2)
            gp.partition_all_reduce(VM[:, :], red[:, 0, :], P, RMAX).then_inc(allred, 1)
            gp.partition_all_reduce(C2[:, :], red[:, 1, :], P, RMAX).then_inc(allred, 1)

            def prep(h, u, first=False):
                if not (first and u == 0):
                    gp.wait_ge(pn_ready, h)
                if not first:
                    gp.wait_ge(g_used, h * NT + (NG - NT))
                    gp.wait_ge(z_ready, h * NV - NV)
                    gp.wait_ge(g_ready, h * NT - NT)
                gp.tensor_copy(KB[:, u, :], S2[:, DS(h, 1), :].rearrange("p o t -> p (o t)")).then_inc(kb_ready, 1)
                seq_h = SEQ[:, :, DS(h, 1), :].rearrange("p t o d -> p t (o d)")
                for e, tab in enumerate((EE, FF)):
                    w = tab[:, DS(h, 1), :].rearrange("p o t -> p (o t)").unsqueeze(2).broadcast_to([P, NT, DV])
                    gp.tensor_tensor(V2[:, :, e, :], seq_h, w, ALU.mult).then_inc(v2_ready, 1)

            def combine(h, first=False):
                gp.wait_ge(bank_free, h * NB + 2 * NB)
                for e, tab in enumerate((AA, BBT)):
                    w = tab[:, DS(h, 1), :].rearrange("p o t -> p (o t)").unsqueeze(2).broadcast_to([P, NT, DV])
                    own.mark(gp.tensor_tensor(T[:, :, e, :], T[:, :, e, :], w, ALU.mult))
                own.wait(gp)
                if not first:
                    gp.wait_ge(hid_done, h)
                gp.tensor_tensor(ND[:, :, :], T[:, :, 0, :], T[:, :, 1, :], ALU.add).then_inc(comb_ready, 1)

            gp.wait_ge(tabs_done, 1)
            prep(0, 0, True)
            prep(1, 1, True)
            gp.wait_ge(deg_done, 1)
            gp.tensor_tensor(DINV[:, :], DINV[:, :], mhalf[:, :], ALU.pow).then_inc(pow_done, 1)
            prep(2, 0)
            combine(0, True)
            own_per = 4
            with gp.Fori(1, H // 2 - 1) as p:
                own.enter(p, 1, own_per)
                for u in range(2):
                    prep(p * 2 + (u + 1), 1 - u)
                    combine(p * 2 + (u - 1))
                own.leave(H // 2 - 1)
            prep(H - 1, 1)
            combine(H - 3)
            combine(H - 2)
            combine(H - 1)

            def rstd_of(t, u, ready, done):
                gp.wait_ge(ready, t + 1)
                gp.tensor_tensor(rstd[:, u:u + 1], vps[:, u:u + 1], mhalf[:, 0:1], ALU.pow).then_inc(done, 1)

            def x_minus_1(t, u):
                gp.wait_ge(xr_in[u], (t - u) * 8 + 16)
                gp.tensor_tensor(xr[:, u, :], xr[:, u, :], mone[:, :].broadcast_to([P, D]), ALU.add).then_inc(xm_done, 1)

            x_minus_1(0, 0)
            x_minus_1(1, 1)
            gp.wait_ge(ne_in, 16)
            own.mark(gp.tensor_tensor(MT[:, :, 0:P], MT[:, :, 0:P], NEB[:, 0:P].unsqueeze(1).broadcast_to([P, NT, P]), ALU.mult))
            gp.wait_ge(ap_in[0], 16)
            own.wait(gp)
            own.mark(gp.tensor_tensor(S2P[:, 0, :, :], APN[:, 0, :, :], MT[:, :, 0:P], ALU.add))
            own.wait(gp)
            gp.tensor_tensor(S2P[:, 0, 0, :], S2P[:, 0, 0, :], id2[:, :], ALU.add).then_inc(s2_done, 1)
            rstd_of(0, 0, var_done, rstd_done)
            rstd_of(1, 1, var_done, rstd_done)
            with gp.Fori(1, NT // 2) as p:
                for u in range(2):
                    x_minus_1(p * 2 + u, u)
                    rstd_of(p * 2 + u, u, var_done, rstd_done)
            with gp.Fori(0, NT // 2) as p:
                for u in range(2):
                    rstd_of(p * 2 + u, u, var2_done, rstd2_done)

        @block.tensor
        def _(pe):
            mm, tr = nc.tensor.matmul, nc.tensor.transpose
            pe.wait_ge(consts, 6)

            def x_transpose(t, u):
                pe.wait_ge(x_in[u], (t - u) * 8 + 16)
                for k in range(KC):
                    last = tr(pb[u][:, k * P:(k + 1) * P], xs[:, u, k * P:(k + 1) * P], idf[:, :])
                last.then_inc(xT_ps, 1)

            def seq_product(t, u, bank_used=True, bank4_used=True, wa=False):
                pe.wait_ge(xT_sb, t + 1)
                if bank_used:
                    pe.wait_ge(seq_sb, t - 1)
                for k in range(KC):
                    last = mm(pb[2 + u][:, :], xT[:, u, k * P:(k + 1) * P], WS[:, k, :], start=(k == 0), stop=(k == KC - 1))
                last.then_inc(seq_ps, 1)
                if wa:
                    pe.wait_ge(wa_done, 1)
                if bank4_used:
                    pe.wait_ge(s_sb, t)
                for k in range(KC):
                    last = mm(pb[4][:, 0:2 * H], xT[:, u, k * P:(k + 1) * P], WA[:, k, :], start=(k == 0), stop=(k == KC - 1))
                last.then_inc(s_ps, 1)

            def mask_tiles(t, u, banks_used=True):
                pe.wait_ge(adjb_done, t + 1)
                for j in range(NT):
                    last = mm(pb[7][:, j:j + 1], adj_b[:, u, j * P:(j + 1) * P], ones[:, 0:1], start=False, stop=True,
                              skip_group_check=True)
                last.then_inc(col_ps, 1)
                pe.wait_ge(mask_done, t + 1)
                for half, (ps, evacuated, bank) in enumerate(((mtA_ps, mtA_sb, 5), (mtB_ps, mtB_sb, 6))):
                    if banks_used:
                        pe.wait_ge(evacuated, t)
                    bk = pb[bank][:, :].bitcast(bf16)
                    for jj in range(HALF):
                        j = half * HALF + jj
                        last = tr(bk[:, jj * P:(jj + 1) * P], mask_b[:, u, j * P:(j + 1) * P], idb[:, :])
                    last.then_inc(ps, 1)

            mm(pb[7][:, 0:NT], MT[:, 0, 0:P], ones[:, :], start=True, stop=True, skip_group_check=True)
            x_transpose(0, 0)
            pe.wait_ge(wseq_in, 16)
            seq_product(0, 0, False, False, wa=True)
            x_transpose(1, 1)
            mask_tiles(0, 0, False)
            seq_product(1, 1, False)
            x_transpose(2, 0)
            mask_tiles(1, 1)
            with pe.Fori(1, NT // 2 - 1) as p:
                for u in range(2):
                    t = p * 2 + u
                    seq_product(t, u)
                    x_transpose(t + 1, 1 - u)
                    mask_tiles(t, u)
            seq_product(NT - 2, 0)
            x_transpose(NT - 1, 1)
            mask_tiles(NT - 2, 0)
            seq_product(NT - 1, 1)
            mask_tiles(NT - 1, 1)

            pe.wait_ge(s_sb, NT)
            pe.wait_ge(seq_sb, NT)
            for t in range(NT):
                last = tr(pb[t // 4][0:H, (t % 4) * P:(t % 4 + 1) * P], S1[:, :, t], idf[:, :])
                if t % 4 == 3:
                    last.then_inc(s1T_ps, 1)
            tr(pb[4][0:NT, 0:P], EMP[:, :], idf[:, :]).then_inc(ne_ps, 1)

            pe.wait_ge(s1T_sb, KC)
            pe.wait_ge(ne_sb, 1)
            pe.wait_ge(mtA_sb, NT)
            pe.wait_ge(mtB_sb, NT)
            pe.sem_inc(g_used, NG)

            with pe.Fori(0, H // 2) as p:
                for u in range(2):
                    h = p * 2 + u
                    pe.wait_ge(pn_ready, h + 1)
                    for j in range(NT):
                        s = (u * NT + j) % NG
                        pe.wait_ge(g_ready, h * NT + (j + 1))
                        for i in range(NT):
                            bank, c = i // IB, (i % IB) * 4 * DV
                            if j == 0 and i % IB == 0:
                                pe.wait_ge(bank_free, h * NB + (bank + 1))
                            mm(pb[bank][:, c:c + 4 * DV], G[:, s, i * P:(i + 1) * P],
                               PN[:, u, j, 0:4, :].rearrange("p c d -> p (c d)"),
                               start=(j == 0 and i % IB == 0), stop=(j == NT - 1), skip_group_check=True)
                            last = mm(pb[bank][:, c + 2 * DV:c + 4 * DV], MT[:, j, i * P:(i + 1) * P],
                                      PN[:, u, j, 4:6, :].rearrange("p c d -> p (c d)"),
                                      start=False, stop=(j == NT - 1), skip_group_check=True)
                        last.then_inc(g_used, 1)

            pe.wait_ge(hid_done, H)
            pe.wait_ge(wout_in, 16)

            def hid_transpose(t, u):
                for k in range(KC):
                    last = tr(pb[u][:, k * P:(k + 1) * P], HC[:, u, k * P:(k + 1) * P], idf[:, :])
                last.then_inc(hT_ps, 1)

            def out_product(t, u, bank_used=True):
                pe.wait_ge(hT_sb, t + 1)
                if bank_used:
                    pe.wait_ge(v_added, t - 1)
                for k in range(KC):
                    last = mm(pb[2 + u][:, :], hT[:, u, k * P:(k + 1) * P], WO[:, k, :], start=(k == 0), stop=(k == KC - 1))
                last.then_inc(o_ps, 1)

            def hid_wait(t):
                pe.wait_ge(hc_done, t + 1)

            for t in range(2):
                hid_wait(t)
                hid_transpose(t, t)
            out_product(0, 0, False)
            hid_wait(2)
            hid_transpose(2, 0)
            out_product(1, 1, False)
            with pe.Fori(1, NT // 2 - 1) as p:
                for u in range(2):
                    hid_wait(p * 2 + (u + 1))
                    hid_transpose(p * 2 + (u + 1), 1 - u)
                    out_product(p * 2 + u, u)
            hid_wait(NT - 1)
            hid_transpose(NT - 1, 1)
            out_product(NT - 2, 0)
            out_product(NT - 1, 1)

            def product(t, u, free, free_at, ready, moving, done, each=None):
                if free is not None:
                    pe.wait_ge(free, free_at)
                pe.wait_ge(ready, t + 1)
                for j in range(NT):
                    if each is not None:
                        pe.wait_ge(each, j + 1)
                    for l in range(2):
                        last = mm(pb[4 + 2 * u + l][:, :], S2P[:, u, j, :], moving[:, l, j, :],
                                  start=(j == 0), stop=(j == NT - 1))
                last.then_inc(done, 1)

            product(0, 0, bank_free, (H + 1) * NB, s2_done, XH, y_ps, each=xl_done)
            product(1, 1, None, 0, s2_done, XH, y_ps)
            with pe.Fori(1, NT // 2) as p:
                for u in range(2):
                    t = p * 2 + u
                    product(t, u, yv_done, t - 1, s2_done, XH, y_ps)
            product(0, 0, yv_done, NT - 1, pan_done, ZH, o2_ps, each=zl_done)
            product(1, 1, yv_done, NT, pan_done, ZH, o2_ps)
            with pe.Fori(1, NT // 2) as p:
                for u in range(2):
                    t = p * 2 + u
                    product(t, u, ov_done, t - 1, pan_done, ZH, o2_ps)

        @block.scalar
        def _(sc):
            A = nc.scalar.activation

            def cast_adj(t, u, fresh=False):
                sc.wait_ge(adj_in[u], (t - u) * 8 + 16)
                if not fresh:
                    sc.wait_ge(col_ps, t - 1)
                    sc.wait_ge(mask_done, t - 1)
                A(adj_b[:, u, :], adj_f[:, u, :], ACT.Copy, accum_out=RS[:, u:u + 1]).then_inc(adjb_done, 1)

            def evacuate(t, u):
                sc.wait_ge(seq_ps, t + 1)
                A(SEQ[:, DS(t, 1), :, 0:DH].rearrange("p o h d -> p (o h) d"),
                  pb[2 + u][:, :].rearrange("p (h d) -> p h d", d=DH), ACT.Copy).then_inc(seq_sb, 1)
                sc.wait_ge(mtA_ps, t + 1)
                A(MT[:, 0:HALF, DS(t * P, P)],
                  pb[5][:, :].bitcast(bf16).rearrange("p (j i) -> p j i", i=P), ACT.Copy).then_inc(mtA_sb, 1)

            cast_adj(0, 0, True)
            cast_adj(1, 1, True)
            evacuate(0, 0)
            with sc.Fori(1, NT // 2) as p:
                for u in range(2):
                    cast_adj(p * 2 + u, u)
                    evacuate(p * 2 + (u - 1), 1 - u)
            evacuate(NT - 1, 1)

            for k in range(KC):
                sc.wait_ge(s1T_ps, k + 1)
                A(s1T[:, k * 512:(k + 1) * 512], pb[k][0:H, :], ACT.Copy, scale=-BIG).then_inc(s1T_sb, 1)
            sc.wait_ge(texp_in, 1)
            A(FF, EE, ACT.Exp, scale=SLOPE).then_inc(act, 1)
            A(AA, AA, ACT.Exp, scale=1.0 - SLOPE).then_inc(act, 1)
            A(BBT, BBT, ACT.Exp, scale=SLOPE - 1.0).then_inc(act, 1)
            sc.wait_ge(act, 3)
            A(EE, EE, ACT.Exp).then_inc(texp_out, 1)

            def low_sums(h, first=False):
                sc.wait_ge(g_used, h * NT + (NT + NG))
                if not first:
                    sc.wait_ge(comb_ready, h)
                for b in range(NB):
                    n = min(IB, NT - b * IB)
                    A(T[:, b * IB:b * IB + n, :, :], sums(b, n)[:, :, :, 1, :], ACT.Copy, scale=UNSPLIT).then_inc(lo_out, 1)

            def high_operands(h, u):
                sc.wait_ge(v2_ready, h * 2 + 2)
                A(PN[:, u, :, 0:5:4, :], V2[:, :, :, :], ACT.Copy, scale=UNSPLIT).then_inc(hi_ready, 1)

            def att_head(h, u, lows=2, first=False, last=False):
                sc.wait_ge(s1b_in[u], (h - u) * 8 + 16)
                sc.wait_ge(kb_ready, h + 1)
                for j in range(NT):
                    if j in ACTZ:
                        n = ACTZ.index(j)
                        if n >= NZ:
                            sc.wait_ge(g_ready, h * NT + (ACTZ[n - NZ] + 1))
                        elif not first:
                            sc.wait_ge(g_ready, h * NT + (ACTZ[n - NZ] + 1 - NT))
                        A(Z[:, (u * NV + n) % NZ, :], S1B[:, u, :], ACT.Relu, bias=KB[:, u, j:j + 1], scale=-1.0).then_inc(z_ready, 1)
                    if j == AT_SUMS and lows:
                        low_sums(h - 1, first=(lows == 1))
                    if j == AT_HIGH and not last:
                        high_operands(h + 1, 1 - u)

            sc.wait_ge(mtA_ps, NT)
            sc.wait_ge(mtB_ps, NT)
            high_operands(0, 0)
            att_head(0, 0, lows=0, first=True)
            att_head(1, 1, lows=1)
            with sc.Fori(1, H // 2 - 1) as p:
                for u in range(2):
                    att_head(p * 2 + u, u)
            att_head(H - 2, 0)
            att_head(H - 1, 1, last=True)
            low_sums(H - 1)

            def move_hT(t, u, fresh=False):
                sc.wait_ge(hT_ps, t + 1)
                if not fresh:
                    sc.wait_ge(o_ps, t - 1)
                A(hT[:, u, :], pb[u][:, :], ACT.Copy).then_inc(hT_sb, 1)

            def copy_hid(t, u, fresh=False):
                if not fresh:
                    sc.wait_ge(hT_ps, t - 1)
                A(HC[:, u, :].rearrange("p (h d) -> p h d", d=DH),
                  SEQ[:, DS(t, 1), :, 0:DH].rearrange("p o h d -> p (o h) d"), ACT.Copy).then_inc(hc_done, 1)

            def elu_exp(t, u):
                sc.wait_ge(v_added, t + 1)
                A(ee[:, u, :], vv[:, u, :], ACT.Exp).then_inc(ex_done, 1)

            def high_x(t, u):
                sc.wait_ge(v2x_done, t + 1)
                A(XH[:, 0, DS(t, 1), :].rearrange("p o d -> p (o d)"), v2x[:, u, :], ACT.Copy, scale=UNSPLIT).then_inc(xh_done, 1)

            sc.wait_ge(g_ready, H * NT)
            sc.wait_ge(hid_done, H)
            sc.wait_ge(g_used, H * NT + NG)
            copy_hid(0, 0, True)
            copy_hid(1, 1, True)
            move_hT(0, 0, True)
            copy_hid(2, 0)
            move_hT(1, 1, True)

            def first_layer(t, u, n=None):
                if n is None or n < NT - 1:
                    move_hT(t + 1, 1 - u)
                if n is None or n < NT - 2:
                    copy_hid(t + 2, u)
                if n is None or n < NT:
                    elu_exp(t, u)
                if n is None or n >= 2:
                    high_x(t - 2, u)

            elu_exp(0, 0)
            first_layer(1, 1, 1)
            with sc.Fori(1, NT // 2 - 1) as p:
                for u in range(2):
                    first_layer(p * 2 + u, u)
            for t in range(NT - 2, NT + 2):
                first_layer(t, t % 2, t)

            def low_y(t, u, fresh=False):
                sc.wait_ge(y_ps, t + 1)
                if not fresh:
                    sc.wait_ge(yv_done, t - 1)
                A(lw[:, u, :], pb[5 + 2 * u][:, :], ACT.Copy, scale=DSL[:, DS(t, 1)]).then_inc(yl_done, 1)

            def high_z(t, u):
                sc.wait_ge(yv_done, t + 1)
                A(ZH[:, 0, DS(t, 1), :].rearrange("p o d -> p (o d)"), yw[:, u, :], ACT.Copy, scale=UNSPLIT).then_inc(zh_done, 1)

            sc.wait_ge(xl_done, NT)
            for u in range(2):
                low_y(u, u, True)
                high_z(u, u)
            with sc.Fori(1, NT // 2) as p:
                for u in range(2):
                    low_y(p * 2 + u, u)
                    high_z(p * 2 + u, u)

            def low_o(t, u, free, free_at):
                sc.wait_ge(o2_ps, t + 1)
                sc.wait_ge(free, free_at)
                A(lw[:, u, :], pb[5 + 2 * u][:, :], ACT.Copy, scale=UNSPLIT / ZS).then_inc(ol_done, 1)

            for u in range(2):
                low_o(u, u, yv_done, NT)
            with sc.Fori(1, NT // 2) as p:
                for u in range(2):
                    low_o(p * 2 + u, u, ov_done, p * 2 + (u - 1))

        @block.vector
        def _(ve):
            V = nc.vector
            own = Steps(dve)
            ve.wait_ge(wseq_in, 16)
            ve.wait_ge(a_in, 32)
            ws_v = WS.rearrange("p k (h d) -> p (k h) d", d=DH)
            for i in range(2):
                own.mark(V.tensor_tensor(WAtmp, ws_v, AV[:, i, :].unsqueeze(1).broadcast_to([P, KC * H, DH]), ALU.mult))
                own.wait(ve)
                own.mark(V.tensor_reduce(WA[:, :, i * H:(i + 1) * H], WAtmp, AX.X, ALU.add))
                own.wait(ve)
            V.memset(KB[:, :, :], 0.0).then_inc(wa_done, 1)

            def move_xT(t, u, fresh=False):
                ve.wait_ge(xT_ps, t + 1)
                if not fresh:
                    ve.wait_ge(s_ps, t - 1)
                V.tensor_copy(xT[:, u, :], pb[u][:, :]).then_inc(xT_sb, 1)

            def prologue_tile(t, u, fresh=False, more=True, more_fresh=False):
                ve.wait_ge(adjb_done, t + 1)
                own.mark(V.tensor_scalar(EMP[:, DS(t, 1)], RS[:, u:u + 1], 0.0, None, ALU.is_equal))
                V.tensor_copy(ROW[:, DS(t, 1)], RS[:, u:u + 1]).then_inc(row_done, 1)
                own.wait(ve)
                if not fresh:
                    ve.wait_ge(mtB_ps, t - 1)
                V.tensor_scalar(mask_b[:, u, :], adj_b[:, u, :], EMP[:, DS(t, 1)], None, ALU.max).then_inc(mask_done, 1)
                ve.wait_ge(s_ps, t + 1)
                V.tensor_copy(TAB[:, 0:2, :, DS(t, 1)].rearrange("p e h o -> p e (h o)"),
                              pb[4][:, 0:2 * H].rearrange("p (e h) -> p e h", e=2)).then_inc(s_sb, 1)
                if more:
                    move_xT(t + 1, 1 - u, more_fresh)
                ve.wait_ge(seq_sb, t + 1)
                V.tensor_reduce(VMT[:, DS(t, 1), :].rearrange("p o h -> p (o h)"),
                                SEQ[:, DS(t, 1), :, 0:DH].rearrange("p o h d -> p (o h) d"), AX.X, ALU.max,
                                apply_absolute_value=True).then_inc(vm_done, 1)
                ve.wait_ge(mtB_ps, t + 1)
                V.tensor_copy(MT[:, HALF:NT, DS(t * P, P)],
                              pb[6][:, :].bitcast(bf16).rearrange("p (j i) -> p j i", i=P)).then_inc(mtB_sb, 1)

            move_xT(0, 0, True)
            prologue_tile(0, 0, fresh=True, more_fresh=True)
            prologue_tile(1, 1, fresh=True)
            with ve.Fori(1, NT // 2 - 1) as p:
                own.enter(p, 1, 2)
                for u in range(2):
                    prologue_tile(p * 2 + u, u)
                own.leave(NT // 2 - 1)
            prologue_tile(NT - 2, 0)
            prologue_tile(NT - 1, 1, more=False)

            ve.wait_ge(vm_done, NT)
            V.tensor_reduce(red[:, 0, :], VMT.rearrange("p t h -> p h t"), AX.X, ALU.max).then_inc(red_done, 1)
            ve.wait_ge(s_sb, NT)
            V.tensor_reduce(red[:, 1, :], S2, AX.X, ALU.max).then_inc(red_done, 1)
            ve.wait_ge(ne_ps, 1)
            V.tensor_scalar(NEr[:, :], pb[4][0:NT, 0:P], -1.0, 1.0, ALU.mult, ALU.add).then_inc(ne_sb, 1)
            ve.wait_ge(col_ps, NT)
            ve.wait_ge(row_done, NT)
            own.mark(V.tensor_tensor(ROW[:, :], pb[7][:, 0:NT], ROW[:, :], ALU.add))
            own.wait(ve)
            own.mark(V.tensor_scalar(ROW[:, :], ROW[:, :], 0.5, 1.0, ALU.mult, ALU.add))
            own.wait(ve)
            V.tensor_scalar(DINV[:, :], ROW[:, :], 1e-30, None, ALU.max).then_inc(deg_done, 1)

            ve.wait_ge(allred, 2)
            c2b = C2[:, :].unsqueeze(2).broadcast_to([P, H, NT])
            own.mark(V.tensor_scalar(VM[:, :], VM[:, :], 1e-30, None, ALU.max))
            own.mark(V.tensor_tensor(EE, S2, c2b, ALU.subtract))
            own.mark(V.tensor_tensor(AA, S1, c2b, ALU.add))
            own.wait(ve)
            own.mark(V.tensor_scalar(BBT, AA, 0.0, None, ALU.max))
            own.wait(ve)
            own.mark(V.tensor_scalar(AA, AA, 0.0, None, ALU.min))
            own.wait(ve)
            V.tensor_scalar(S2, S2, BIG, None, ALU.mult).then_inc(texp_in, 1)
            own.mark(V.tensor_copy(SEQ[:, :, :, DH], VM[:, :].unsqueeze(1).broadcast_to([P, NT, H])))
            own.mark(V.reciprocal(RV[:, :], VM[:, :]))
            own.wait(ve)
            own.mark(V.tensor_scalar(RV[:, :], RV[:, :], TOP * SPLIT, None, ALU.mult))
            own.wait(ve)
            rvb = RV[:, :].unsqueeze(2).broadcast_to([P, H, NT])
            ve.wait_ge(texp_out, 1)
            own.mark(V.tensor_tensor(EE, EE, rvb, ALU.mult))
            own.mark(V.tensor_tensor(FF, FF, rvb, ALU.mult))
            own.wait(ve)
            V.memset(RD[:, :], 1.0).then_inc(tabs_done, 1)

            def low_operands(h, u):
                ve.wait_ge(hi_ready, h + 1)
                own.mark(V.scalar_tensor_tensor(PN[:, u, :, 1, :], PN[:, u, :, 0, :], -SPLIT, V2[:, :, 0, :], ALU.mult, ALU.add))
                own.mark(V.scalar_tensor_tensor(PN[:, u, :, 5, :], PN[:, u, :, 4, :], -SPLIT, V2[:, :, 1, :], ALU.mult, ALU.add))
                own.wait(ve)
                V.tensor_scalar(PN[:, u, :, 2:4, :].rearrange("p t c d -> p t (c d)"),
                                PN[:, u, :, 4:6, :].rearrange("p t c d -> p t (c d)"), -1.0, None, ALU.mult).then_inc(pn_ready, 1)

            def high_sums(h):
                for b in range(NB):
                    n = min(IB, NT - b * IB)
                    ve.wait_ge(lo_out, h * NB + (b + 1))
                    V.tensor_tensor(T[:, b * IB:b * IB + n, :, :], sums(b, n)[:, :, :, 0, :], T[:, b * IB:b * IB + n, :, :],
                                    ALU.add).then_inc(bank_free, 1)

            def hidden_head(h):
                ve.wait_ge(comb_ready, h + 1)
                own.mark(V.reciprocal(RD[:, :], ND[:, :, DH]))
                own.wait(ve)
                V.scalar_tensor_tensor(SEQ[:, :, DS(h, 1), 0:DH].rearrange("p t o d -> p t (o d)"), ND[:, :, 0:DH],
                                       VM[:, DS(h, 1)], RD[:, :].unsqueeze(2).broadcast_to([P, NT, DH]),
                                       ALU.mult, ALU.mult).then_inc(hid_done, 1)

            def att_head(h, u, first=False, last=False):
                ve.wait_ge(s1b_in[u], (h - u) * 8 + 16)
                ve.wait_ge(kb_ready, h + 1)
                for j in range(NT):
                    s = (u * NT + j) % NG
                    ve.wait_ge(g_used, h * NT + (j + 1))
                    if j in ACTZ:
                        n = ACTZ.index(j)
                        ve.wait_ge(z_ready, h * NV + (n + 1))
                        V.tensor_tensor(G[:, s, :], Z[:, (u * NV + n) % NZ, :], MT[:, j, :], ALU.min).then_inc(g_ready, 1)
                    else:
                        V.scalar_tensor_tensor(G[:, s, :], S1B[:, u, :], KB[:, u, j:j + 1], MT[:, j, :],
                                               ALU.is_lt, ALU.mult).then_inc(g_ready, 1)
                    if j == AT_SUMS and not first:
                        high_sums(h - 1)
                    if j == AT_LOW and not last:
                        low_operands(h + 1, 1 - u)
                    if j == AT_HID and not first:
                        hidden_head(h - 1)

            ve.wait_ge(adjb_done, NT)
            low_operands(0, 0)
            ve.sem_inc(bank_free, NB)
            att_head(0, 0, first=True)
            att_head(1, 1)
            ve.wait_ge(pow_done, 1)
            own.mark(V.scalar_tensor_tensor(DINV[:, :], ROW[:, :], 0.0, DINV[:, :], ALU.is_gt, ALU.mult))
            own.wait(ve)
            V.tensor_scalar(DSX[:, :], DINV[:, :], XS * SPLIT, None, ALU.mult).then_inc(dscale, 1)
            V.tensor_scalar(DSZ[:, :], DINV[:, :], 0.5 / XS * ZS * SPLIT, None, ALU.mult).then_inc(dscale, 1)
            V.tensor_scalar(DSL[:, :], DINV[:, :], 0.5 / XS * ZS, None, ALU.mult).then_inc(dscale, 1)
            ve.wait_ge(dscale, 3)
            with ve.Fori(1, H // 2 - 1) as p:
                own.enter(p, 1, 6)
                for u in range(2):
                    att_head(p * 2 + u, u)
                own.leave(H // 2 - 1)
            att_head(H - 2, 0)
            att_head(H - 1, 1, last=True)
            high_sums(H - 1)
            hidden_head(H - 1)

            ve.wait_ge(bb_in, 16)

            def norm_stats(src, u, done, between):
                own.mark(V.bn_stats(bst[:, u, :], src))
                own.wait(ve)
                between()
                own.mark(V.bn_aggr(mv[:, u, :], bst[:, u, :]))
                own.wait(ve)
                V.tensor_scalar(vps[:, u:u + 1], mv[:, u, 1:2], EPS, None, ALU.add).then_inc(done, 1)

            def add_bias(t, u):
                ve.wait_ge(o_ps, t + 1)
                V.tensor_tensor(vv[:, u, :], pb[2 + u][:, :], BB, ALU.add).then_inc(v_added, 1)

            def low_x(t, u):
                ve.wait_ge(xh_done, t + 1)
                xt = lambda l: XH[:, l, DS(t, 1), :].rearrange("p o d -> p (o d)")
                V.scalar_tensor_tensor(xt(1), xt(0), -SPLIT, v2x[:, u, :], ALU.mult, ALU.add).then_inc(xl_done, 1)

            def elu_and_add(t, u, between):
                ve.wait_ge(v_added, t + 1)
                ve.wait_ge(xm_done, t + 1)
                own.mark(V.scalar_tensor_tensor(rr[:, u, :], vv[:, u, :], 0.0, xr[:, u, :], ALU.max, ALU.add))
                own.wait(ve)
                ve.wait_ge(ex_done, t + 1)
                own.mark(V.scalar_tensor_tensor(rr[:, u, :], ee[:, u, :], 1.0, rr[:, u, :], ALU.min, ALU.add))
                own.wait(ve)
                norm_stats(rr[:, u, :], u, var_done, between)

            def normalise(t, u):
                ve.wait_ge(rstd_done, t + 1)
                ve.wait_ge(hc_done, t + 1)
                x1 = X1[:, DS(t, 1), 0:D].rearrange("p o d -> p (o d)")
                own.mark(V.tensor_scalar(x1, rr[:, u, :], mv[:, u, 0:1], rstd[:, u:u + 1], ALU.subtract, ALU.mult))
                own.wait(ve)
                V.tensor_scalar(v2x[:, u, :], x1, DSX[:, DS(t, 1)], None, ALU.mult).then_inc(v2x_done, 1)

            def first_layer(t, u, n=None):
                if n is None or n < NT:
                    add_bias(t, u)
                if n is None or 3 <= n:
                    low_x(t - 3, 1 - u)
                def before():
                    if n is None or 2 <= n < NT + 2:
                        normalise(t - 2, u)

                if n is None or 1 <= n <= NT:
                    elu_and_add(t - 1, 1 - u, before)
                else:
                    before()

            for t in range(4):
                first_layer(t, t % 2, t)
            with ve.Fori(2, NT // 2) as p:
                own.enter(p, 2, 10)
                for u in range(2):
                    first_layer(p * 2 + u, u)
                own.leave(NT // 2)
            for t in range(NT, NT + 3):
                first_layer(t, t % 2, t)

            def restore_and_add(t, u, fresh=False):
                mt = MT[:, :, DS(t * P, P)]
                own.mark(V.tensor_tensor(mt, mt, NEB[:, DS(t * P, P)].unsqueeze(1).broadcast_to([P, NT, P]), ALU.mult))
                own.wait(ve)
                ve.wait_ge(ap_in[u], (t - u) * 8 + 16)
                if not fresh:
                    ve.wait_ge(y_ps, t - 1)
                own.mark(V.tensor_tensor(S2P[:, u, :, :], APN[:, u, :, :], mt, ALU.add))
                own.wait(ve)
                diag = S2P[:, u, DS(t, 1), :].rearrange("p o i -> p (o i)")
                V.tensor_tensor(diag, diag, id2[:, :], ALU.add).then_inc(s2_done, 1)

            def z_sum(t, u, fresh=False):
                ve.wait_ge(yl_done, t + 1)
                if not fresh:
                    ve.wait_ge(zl_done, t - 1)
                V.scalar_tensor_tensor(yw[:, u, :], pb[4 + 2 * u][:, :], DSZ[:, DS(t, 1)], lw[:, u, :],
                                       ALU.mult, ALU.add).then_inc(yv_done, 1)

            def low_z(t, u):
                ve.wait_ge(zh_done, t + 1)
                zt = lambda l: ZH[:, l, DS(t, 1), :].rearrange("p o d -> p (o d)")
                V.scalar_tensor_tensor(zt(1), zt(0), -SPLIT, yw[:, u, :], ALU.mult, ALU.add).then_inc(zl_done, 1)

            def copy_panel(t, u, free, free_at):
                ve.wait_ge(free, free_at)
                V.tensor_copy(S2P[:, u, :, :], MT[:, :, DS(t * P, P)]).then_inc(pan_done, 1)

            ve.wait_ge(ne_in, 16)
            restore_and_add(1, 1, True)
            for t in range(2):
                z_sum(t, t, True)
                low_z(t, t)
                restore_and_add(t + 2, t)
            with ve.Fori(1, NT // 2 - 1) as p:
                own.enter(p, 1, 4)
                for u in range(2):
                    t = p * 2 + u
                    z_sum(t, u)
                    low_z(t, u)
                    restore_and_add(t + 2, u)
                own.leave(NT // 2 - 1)
            z_sum(NT - 2, 0)
            low_z(NT - 2, 0)
            copy_panel(0, 0, y_ps, NT - 1)
            z_sum(NT - 1, 1)
            low_z(NT - 1, 1)
            copy_panel(1, 1, y_ps, NT)

            def o_sum(t, u, between, fresh=False):
                ve.wait_ge(ol_done, t + 1)
                if not fresh:
                    ve.wait_ge(out_st[u], (t - u) * 8)
                own.mark(V.scalar_tensor_tensor(yw[:, u, :], pb[4 + 2 * u][:, :], 1.0 / ZS, lw[:, u, :], ALU.mult, ALU.add))
                own.wait(ve)
                V.tensor_tensor(yw[:, u, :], yw[:, u, :], X1[:, DS(t, 1), 0:D].rearrange("p o d -> p (o d)"), ALU.add).then_inc(ov_done, 1)
                ve.wait_ge(ov_done, t + 1)
                norm_stats(yw[:, u, :], u, var2_done, between)

            def o_norm(t, u):
                ve.wait_ge(rstd2_done, t + 1)
                V.tensor_scalar(yw[:, u, :], yw[:, u, :], mv[:, u, 0:1], rstd[:, u:u + 1], ALU.subtract, ALU.mult).then_inc(out_ready, 1)

            for t in range(2):
                o_sum(t, t, lambda: copy_panel(t + 2, t, o2_ps, t + 1), True)
                o_norm(t, t)
            with ve.Fori(1, NT // 2 - 1) as p:
                own.enter(p, 1, 6)
                for u in range(2):
                    t = p * 2 + u
                    o_sum(t, u, lambda: copy_panel(t + 2, u, o2_ps, t + 1))
                    o_norm(t, u)
                own.leave(NT // 2 - 1)
            for t in (NT - 2, NT - 1):
                o_sum(t, t % 2, lambda: None)
                o_norm(t, t % 2)


_INS = ['x', 'adj', 'L0_gnn_W_seq', 'L0_gnn_a1', 'L0_gnn_a2', 'L0_gnn_W_out', 'L0_gnn_b_out']
_OUTS = [((2048, 512), 'float32')]


def kernel(**inputs):
    import numpy as _np
    import concourse.bacc as _bacc
    from concourse import mybir as _mybir
    from concourse.bass_utils import run_bass_kernel_spmd as _run

    nc = _bacc.Bacc("TRN2", target_bir_lowering=False, num_devices=1)
    arrays, args = {}, []
    for name in _INS:
        a = _np.ascontiguousarray(inputs[name])
        arrays[f"in_{name}_dram"] = a
        args.append(nc.dram_tensor(f"in_{name}_dram", a.shape, _mybir.dt.from_np(a.dtype), kind="ExternalInput").ap())
    for i, (shape, dtype) in enumerate(_OUTS):
        dt = _mybir.dt.from_np(_np.dtype(dtype))
        args.append(nc.dram_tensor(f"out_{i}_dram", shape, dt, kind="ExternalOutput").ap())
    args.append(nc.dram_tensor("s1_rows_dram", (16, 2048), _mybir.dt.float32, kind="Internal").ap())
    args.append(nc.dram_tensor("nonempty_dram", (2048,), _mybir.dt.bfloat16, kind="Internal").ap())
    gat_then_normalised_adjacency(nc, *args)
    r = _run(nc, [arrays], core_ids=[0])
    return r.results[0]["out_0_dram"]
```

```python
import numpy as np
import concourse.bass as bass
from concourse import mybir
from contextlib import ExitStack


def gat_then_normalised_adjacency(nc, x, adj, w_seq, a1, a2, w_out, b_out, out, s1_rows, nonempty_row, seq_copy):
    f32, bf16, f16 = mybir.dt.float32, mybir.dt.bfloat16, mybir.dt.float16
    ALU, ACT, AX = mybir.AluOpType, mybir.ActivationFunctionType, mybir.AxisListType

    P = 128
    N, D = x.shape
    NT = N // P
    H = 16
    DH = D // H
    DV = DH + 1
    KC = D // P
    SLOPE = 0.2
    MASKED = -65500.0
    EPS = 1e-5
    BIG = 2.0 ** 60
    SPLIT = 2.0 ** 11
    UNSPLIT = 1.0 / SPLIT
    TOP = 2.0 ** 14
    XS = 2.0 ** 9
    ZS = 2.0 ** 4
    SPREAD = 17.0
    NG = 8
    NZ = 4
    DIRECT = (3, 7, 11, 15)
    SHARED = 15
    SC = 768
    NV = NT - len(DIRECT)
    IB = 3
    NB = -(-NT // IB)
    HALF = NT // 2
    ACTZ = [j for j in range(NT) if j not in DIRECT]
    AT_SUMS, AT_HIGH, AT_LOW, AT_HID = 5, 8, 10, 13
    assert (2 * NV) % NZ == 0 and (2 * NT) % NG == 0

    ctx = ExitStack()
    with ctx:
        def sb(name, shape, dt):
            return ctx.enter_context(nc.sbuf_tensor(name, shape, dt))

        def sem(name):
            return ctx.enter_context(nc.semaphore(name))

        MT = sb("MT", [P, NT, N], bf16)
        SEQ = sb("SEQ", [P, NT, H, DV], f32)
        X1 = SEQ[:, :, :, :].rearrange("p t h d -> p t (h d)")
        RG = sb("RG", [P, 8192], f32)
        adj_f = RG[:, 0:2 * N].rearrange("p (u n) -> p u n", u=2)
        G = RG[:, :].bitcast(bf16).rearrange("p (s n) -> p s n", s=NG)
        XH = RG[:, :].bitcast(f16).rearrange("p (l t d) -> p l t d", l=2, t=NT)
        RZ = sb("RZ", [P, 8192], f32)
        ZH = RZ[:, :].bitcast(f16).rearrange("p (l t d) -> p l t d", l=2, t=NT)
        Z = RZ[:, 0:4096].bitcast(bf16).rearrange("p (s n) -> p s n", s=NZ)
        ZS1 = sb("ZS1", [P, SC], bf16)
        S1B = RZ[:, 4096:8192].rearrange("p (u n) -> p u n", u=2)
        adj_b = RZ[:, 0:2048].bitcast(bf16).rearrange("p (u n) -> p u n", u=2)
        mask_b = RZ[:, 2048:4096].bitcast(bf16).rearrange("p (u n) -> p u n", u=2)
        WS = RZ[:, 4096:6144].rearrange("p (k d) -> p k d", k=KC)
        xs = RZ[:, 6144:7168].rearrange("p (u d) -> p u d", u=2)
        xT = RZ[:, 7168:8192].rearrange("p (u d) -> p u d", u=2)
        WO = RZ[:, 4096:6144].rearrange("p (k d) -> p k d", k=KC)
        wk = RZ[:, 0:4096].rearrange("p (b u d) -> p b u d", b=4, u=2)
        hT, xr, vv, ee = wk[:, 0], wk[:, 1], wk[:, 2], wk[:, 3]
        wk2 = RZ[:, 6144:8192].rearrange("p (b u d) -> p b u d", b=2, u=2)
        rr, v2x = wk2[:, 0], wk2[:, 1]
        PNB = 2 * NT * 6 * DV
        RP = sb("RP", [P, 3 * NT * P], f32)
        assert PNB // 2 + NT * 5 * DV <= 3 * NT * P
        PN = RP[:, 0:PNB // 2].bitcast(f16).rearrange("p (u t c d) -> p u t c d", u=2, t=NT, c=6)
        o = PNB // 2
        T = RP[:, o:o + NT * 2 * DV].rearrange("p (t e d) -> p t e d", t=NT, e=2)
        o += NT * 2 * DV
        V2 = RP[:, o:o + NT * 2 * DV].rearrange("p (t e d) -> p t e d", t=NT, e=2)
        o += NT * 2 * DV
        ND = RP[:, o:o + NT * DV].rearrange("p (t d) -> p t d", t=NT)
        CSA = RP[:, PNB // 4:PNB // 4 + N // 2].bitcast(bf16)
        APN = RP[:, 0:2 * NT * P].rearrange("p (u t i) -> p u t i", u=2, t=NT)
        S2P = RP[:, 2 * NT * P:3 * NT * P].bitcast(bf16).rearrange("p (u t i) -> p u t i", u=2, t=NT)
        W5 = sb("W5", [P, 4, D], f32)
        WAtmp = W5[:, :, :].rearrange("p k (h d) -> p (k h) d", d=DH)
        BB = W5[:, 0, :]
        HC = W5[:, 2:4, :]
        s1T = W5[0:H, :, :].rearrange("p k d -> p (k d)")
        lw, yw = W5[:, 0:2, :], W5[:, 2:4, :]
        idf = sb("idf", [P, P], f32)
        idb = sb("idb", [P, P], bf16)
        id2 = sb("id2", [P, P], bf16)
        mone = sb("mone", [P, 1], f32)
        ones = sb("ones", [P, NT], bf16)
        NEB = sb("NEB", [P, N], bf16)
        TAB = sb("TAB", [P, 6, H, NT], f32)
        S1, S2, EE, FF, AA, BBT = (TAB[:, i] for i in range(6))
        VMT = T[:, :, 0, 0:H]
        VC = sb("VC", [P, 2 * H], f32)
        VM, C2 = VC[:, 0:H], VC[:, H:2 * H]
        RV = sb("RV", [P, H], f32)
        red = sb("red", [P, 2, H], f32)
        WID = sb("WID", [P, 4], f32)
        FLAG = sb("FLAG", [P, 1], mybir.dt.int32)
        S2B, SCO, ADJ, WT = (RG[:, i * N:(i + 1) * N] for i in range(4))
        onesf, S2C, NEGM, RES = RP[:, 0:P], RP[:, P:P + NT], RP[:, P + NT:P + NT + 1], RP[:, 2 * P:2 * P + NT * DV].rearrange("p (t d) -> p t d", t=NT)
        KB = sb("KB", [P, 2, NT], f32)
        RS = sb("RS", [P, 2], f32)
        ROW = sb("ROW", [P, NT], f32)
        EMP = sb("EMP", [P, NT], f32)
        DINV = sb("DINV", [P, NT], f32)
        DSX = sb("DSX", [P, NT], f32)
        DSZ = sb("DSZ", [P, NT], f32)
        DSL = sb("DSL", [P, NT], f32)
        NEr = sb("NEr", [NT, P], bf16)
        RD = sb("RD", [P, NT], f32)
        AV = sb("AV", [P, 2, DH], f32)
        WA = sb("WA", [P, KC, 2 * H], f32)
        bst = sb("bst", [P, 2, 6], f32)
        mv = sb("mv", [P, 2, 2], f32)
        vps = sb("vps", [P, 2], f32)
        rstd = sb("rstd", [P, 2], f32)
        mhalf = sb("mhalf", [P, NT], f32)

        RMAX = bass.bass_isa.ReduceOp.max
        pb = [ctx.enter_context(nc.psum_tensor(f"bank{i}", [P, 512], f32)) for i in range(8)]

        consts = sem("consts")
        wseq_in = sem("wseq_in")
        a_in = sem("a_in")
        x_in = [sem(f"x_in{u}") for u in range(2)]
        adj_in = [sem(f"adj_in{u}") for u in range(2)]
        xT_ps = sem("xT_ps")
        xT_sb = sem("xT_sb")
        wa_done = sem("wa_done")
        seq_ps = sem("seq_ps")
        s_ps = sem("s_ps")
        seq_sb = sem("seq_sb")
        s_sb = sem("s_sb")
        adjb_done = sem("adjb_done")
        mask_done = sem("mask_done")
        col_ps = sem("col_ps")
        tiles_added = sem("tiles_added")
        mtA_ps = sem("mtA_ps")
        mtB_ps = sem("mtB_ps")
        mtA_sb = sem("mtA_sb")
        mtB_sb = sem("mtB_sb")
        dve = sem("dve_step")
        pool = sem("pool_step")
        act = sem("act_step")
        vm_done = sem("vm_done")
        red_done = sem("red_done")
        allred = sem("allred")
        seq_stored = sem("seq_stored")
        spread_done = sem("spread_done")
        flag_ready = sem("flag_ready")
        gen_seq_in = sem("gen_seq_in")
        gen_adj_in = sem("gen_adj_in")
        gen_diag = sem("gen_diag")
        gen_s2_ps = sem("gen_s2_ps")
        gen_s2_sb = sem("gen_s2_sb")
        gen_sum = sem("gen_sum")
        gen_leaky = sem("gen_leaky")
        gen_scores = sem("gen_scores")
        gen_max = sem("gen_max")
        gen_exp = sem("gen_exp")
        gen_wt_ps = sem("gen_wt_ps")
        gen_wt_sb = sem("gen_wt_sb")
        gen_res_ps = sem("gen_res_ps")
        gen_res = sem("gen_res")
        gen_rcp = sem("gen_rcp")
        gen_head = sem("gen_head")
        s1T_ps = sem("s1T_ps")
        s1T_sb = sem("s1T_sb")
        s1_stored = sem("s1_stored")
        texp_in = sem("texp_in")
        texp_out = sem("texp_out")
        tabs_done = sem("tabs_done")
        ne_sb = sem("ne_sb")
        ne_stored = sem("ne_stored")
        ne_in = sem("ne_in")
        ne_ps = sem("ne_ps")
        s1b_in = [sem(f"s1b_in{u}") for u in range(2)]
        kb_ready = sem("kb_ready")
        v2_ready = sem("v2_ready")
        hi_ready = sem("hi_ready")
        pn_ready = sem("pn_ready")
        z_ready = sem("z_ready")
        zs_ready = sem("zs_ready")
        g_ready = sem("g_ready")
        g_used = sem("g_used")
        lo_out = sem("lo_out")
        bank_free = sem("bank_free")
        comb_ready = sem("comb_ready")
        hid_done = sem("hid_done")
        hc_done = sem("hc_done")
        deg_done = sem("deg_done")
        pow_done = sem("pow_done")
        row_done = sem("row_done")
        dscale = sem("dscale")
        wout_in = sem("wout_in")
        bb_in = sem("bb_in")
        xr_in = [sem(f"xr_in{u}") for u in range(2)]
        hT_ps = sem("hT_ps")
        hT_sb = sem("hT_sb")
        o_ps = sem("o_ps")
        xm_done = sem("xm_done")
        v_added = sem("v_added")
        ex_done = sem("ex_done")
        xr_used = sem("xr_used")
        var_done = sem("var_done")
        rstd_done = sem("rstd_done")
        x1_done = sem("x1_done")
        v2x_done = sem("v2x_done")
        xh_done = sem("xh_done")
        xl_done = sem("xl_done")
        ap_in = [sem(f"ap_in{u}") for u in range(2)]
        s2_done = sem("s2_done")
        y_ps = sem("y_ps")
        yl_done = sem("yl_done")
        yv_done = sem("yv_done")
        zh_done = sem("zh_done")
        zl_done = sem("zl_done")
        pan_done = sem("pan_done")
        o2_ps = sem("o2_ps")
        ol_done = sem("ol_done")
        var2_done = sem("var2_done")
        rstd2_done = sem("rstd2_done")
        ov_done = sem("ov_done")
        out_ready = sem("out_ready")
        out_st = [sem(f"out_st{u}") for u in range(2)]

        class Steps:

            def __init__(self, s):
                self.s, self.n, self.made = s, 0, 0

            def mark(self, ins):
                ins.then_inc(self.s, 1)
                self.n = self.n + 1
                self.made = self.made + 1

            def wait(self, eng):
                eng.wait_ge(self.s, self.n)

            def enter(self, i, start, per):
                self.base, self.start, self.per, self.made = self.n, start, per, 0
                self.n = i * per + (self.base - start * per)

            def leave(self, end):
                assert self.made == self.per
                self.n = self.base + (end - self.start) * self.per

        block = ctx.enter_context(nc.Block())
        DS = bass.ds

        def sums(b, n):
            return pb[b][:, 0:n * 4 * DV].rearrange("p (i e l d) -> p i e l d", i=n, e=2, l=2)

        @block.sync
        def _(sp):
            sp.dma_start(WS, w_seq.rearrange("(k p) d -> p k d", p=P)).then_inc(wseq_in, 16)
            for i, a in enumerate((a1, a2)):
                sp.dma_start(AV[:, i, :], a.rearrange("(o d) -> o d", o=1).broadcast_to([P, DH])).then_inc(a_in, 16)

            def load_x(t, u):
                sp.dma_start(xs[:, u, :], x[DS(t * P, P), :]).then_inc(x_in[u], 16)

            def load_adj(t, u):
                sp.dma_start(adj_f[:, u, :], adj[DS(t * P, P), :]).then_inc(adj_in[u], 16)

            for u in range(2):
                load_x(u, u)
                load_adj(u, u)
            with sp.Fori(1, NT // 2) as p:
                for u in range(2):
                    t = p * 2 + u
                    sp.wait_ge(xT_ps, t - 1)
                    load_x(t, u)
                    sp.wait_ge(adjb_done, t - 1)
                    load_adj(t, u)
            sp.wait_ge(s1T_sb, KC)
            sp.dma_start(s1_rows[:, :], s1T).then_inc(s1_stored, 16)
            sp.wait_ge(ne_sb, 1)
            sp.dma_start(nonempty_row.rearrange("(t p) -> t p", p=P), NEr[:, :]).then_inc(ne_stored, 16)
            sp.wait_ge(s1_stored, 16)

            def load_s1(h, u):
                sp.dma_start(S1B[:, u, :], s1_rows[DS(h, 1), :].broadcast_to([P, N])).then_inc(s1b_in[u], 16)

            sp.wait_ge(s_ps, NT)
            load_s1(0, 0)
            load_s1(1, 1)
            sp.wait_ge(ne_stored, 16)
            sp.dma_start(NEB[:, :], nonempty_row.rearrange("(o n) -> o n", o=1).broadcast_to([P, N])).then_inc(ne_in, 16)
            sp.wait_ge(tabs_done, 1)
            sp.dma_start(seq_copy[:, :], SEQ[:, :, :, :].rearrange("p t h d -> p (t h d)")).then_inc(seq_stored, 16)
            with sp.Fori(1, H // 2) as p:
                for u in range(2):
                    h = p * 2 + u
                    sp.wait_ge(z_ready, h * NV - NV)
                    sp.wait_ge(g_ready, h * NT - NT)
                    load_s1(h, u)
            sp.wait_ge(z_ready, (H - 1) * NV)
            sp.wait_ge(g_ready, (H - 1) * NT)
            sp.dma_start(WO, w_out.rearrange("(k p) d -> p k d", p=P)).then_inc(wout_in, 16)
            sp.dma_start(BB, b_out.rearrange("(o d) -> o d", o=1).broadcast_to([P, D])).then_inc(bb_in, 16)

            def load_xr(t, u):
                sp.dma_start(xr[:, u, :], x[DS(t * P, P), :]).then_inc(xr_in[u], 16)

            def load_ap(t, u):
                sp.dma_start(APN[:, u, :, :],
                             adj.rearrange("(t p) i -> p t i", p=P)[:, :, DS(t * P, P)]).then_inc(ap_in[u], 16)

            def general_loads():
                sp.wait_ge(hid_done, H)
                sp.wait_ge(g_used, H * NT + NG)
                sp.dma_start(SEQ[:, :, :, :].rearrange("p t h d -> p (t h d)"), seq_copy[:, :]).then_inc(gen_seq_in, 16)
                with sp.Fori(0, H) as h:
                    with sp.Fori(0, NT) as t:
                        sp.wait_ge(gen_scores, h * NT + t + 1)
                        sp.dma_start(ADJ, adj[DS(t * P, P), :]).then_inc(gen_adj_in, 16)
                sp.wait_ge(gen_head, H)

            sp.wait_ge(g_ready, H * NT)
            for u in range(2):
                load_xr(u, u)
            sp.wait_ge(flag_ready, 1)
            with sp.If(sp.value_load(FLAG[0:1, 0:1], min_val=0, max_val=1) > 0):
                general_loads()

            sp.wait_ge(g_used, H * NT + NG)
            load_ap(0, 0)
            sp.wait_ge(hid_done, H)
            load_ap(1, 1)
            with sp.Fori(1, NT // 2) as p:
                for u in range(2):
                    t = p * 2 + u
                    sp.wait_ge(xr_used, t - 1)
                    load_xr(t, u)
            with sp.Fori(1, NT // 2) as p:
                for u in range(2):
                    t = p * 2 + u
                    sp.wait_ge(s2_done, t - 1)
                    load_ap(t, u)
            with sp.Fori(0, NT // 2) as p:
                for u in range(2):
                    t = p * 2 + u
                    sp.wait_ge(out_ready, t + 1)
                    sp.dma_start(out[DS(t * P, P), :], yw[:, u, :]).then_inc(out_st[u], 16)
            for u in range(2):
                sp.wait_ge(out_st[u], 16 * (NT // 2))

        @block.gpsimd
        def _(gp):
            own = Steps(pool)
            own.mark(gp.memset(idf[:, :], 0.0))
            own.mark(gp.memset(idb[:, :], 0.0))
            own.mark(gp.memset(id2[:, :], 0.0))
            own.mark(gp.memset(mone[:, :], -1.0))
            gp.memset(ones[:, :], 1.0).then_inc(consts, 1)
            gp.memset(CSA, 0.0).then_inc(consts, 1)
            gp.memset(mhalf[:, :], -0.5).then_inc(consts, 1)
            own.wait(gp)
            for m, one in ((idf, 1.0), (idb, 1.0), (id2, 2.0)):
                gp.affine_select(out=m[:, :], in_=m[:, :], compare_op=ALU.not_equal, fill=one, base=0,
                                 pattern=[[-1, P]], channel_multiplier=1).then_inc(consts, 1)
            gp.wait_ge(red_done, 2)
            gp.partition_all_reduce(VC[:, :], red[:, :, :].rearrange("p e h -> p (e h)"), P, RMAX).then_inc(allred, 1)

            def prep(h, u, first=False):
                if not (first and u == 0):
                    gp.wait_ge(pn_ready, h)
                if not first:
                    gp.wait_ge(g_used, h * NT + (NG - NT))
                    gp.wait_ge(z_ready, h * NV - NV)
                    gp.wait_ge(g_ready, h * NT - NT)
                gp.tensor_copy(KB[:, u, :], S2[:, DS(h, 1), :].rearrange("p o t -> p (o t)")).then_inc(kb_ready, 1)
                seq_h = SEQ[:, :, DS(h, 1), :].rearrange("p t o d -> p t (o d)")
                for e, tab in enumerate((EE, FF)):
                    w = tab[:, DS(h, 1), :].rearrange("p o t -> p (o t)").unsqueeze(2).broadcast_to([P, NT, DV])
                    gp.tensor_tensor(V2[:, :, e, :], seq_h, w, ALU.mult).then_inc(v2_ready, 1)

            def combine(h, first=False):
                gp.wait_ge(bank_free, h * NB + 2 * NB)
                for e, tab in enumerate((AA, BBT)):
                    w = tab[:, DS(h, 1), :].rearrange("p o t -> p (o t)").unsqueeze(2).broadcast_to([P, NT, DV])
                    own.mark(gp.tensor_tensor(T[:, :, e, :], T[:, :, e, :], w, ALU.mult))
                own.wait(gp)
                if not first:
                    gp.wait_ge(hid_done, h)
                gp.tensor_tensor(ND[:, :, :], T[:, :, 0, :], T[:, :, 1, :], ALU.add).then_inc(comb_ready, 1)

            gp.wait_ge(tabs_done, 1)
            prep(0, 0, True)
            prep(1, 1, True)
            prep(2, 0)
            combine(0, True)
            gp.wait_ge(deg_done, 1)
            gp.tensor_tensor(DINV[:, :], DINV[:, :], mhalf[:, :], ALU.pow).then_inc(pow_done, 1)
            own_per = 4
            with gp.Fori(1, H // 2 - 1) as p:
                own.enter(p, 1, own_per)
                for u in range(2):
                    prep(p * 2 + (u + 1), 1 - u)
                    combine(p * 2 + (u - 1))
                own.leave(H // 2 - 1)
            prep(H - 1, 1)
            combine(H - 3)
            combine(H - 2)
            gp.wait_ge(spread_done, 1)
            own.mark(gp.partition_all_reduce(WID[:, 3:4], WID[:, 2:3], P, RMAX))
            own.wait(gp)
            gp.tensor_copy(FLAG[:, :], WID[:, 3:4]).then_inc(flag_ready, 1)

            def rstd_of(t, u, ready, done):
                gp.wait_ge(ready, t + 1)
                gp.tensor_tensor(rstd[:, u:u + 1], vps[:, u:u + 1], mhalf[:, 0:1], ALU.pow).then_inc(done, 1)

            def x_minus_1(t, u):
                gp.wait_ge(xr_in[u], (t - u) * 8 + 16)
                gp.tensor_tensor(xr[:, u, :], xr[:, u, :], mone[:, :].broadcast_to([P, D]), ALU.add).then_inc(xm_done, 1)

            x_minus_1(0, 0)
            x_minus_1(1, 1)
            gp.wait_ge(ne_in, 16)
            gp.wait_ge(g_used, H * NT + NG)
            own.mark(gp.tensor_tensor(MT[:, :, P:2 * P], MT[:, :, P:2 * P], NEB[:, P:2 * P].unsqueeze(1).broadcast_to([P, NT, P]), ALU.mult))
            gp.wait_ge(ap_in[1], 16)
            own.wait(gp)
            own.mark(gp.tensor_tensor(S2P[:, 1, :, :], APN[:, 1, :, :], MT[:, :, P:2 * P], ALU.add))
            own.wait(gp)
            gp.wait_ge(s2_done, 1)
            gp.tensor_tensor(S2P[:, 1, 1, :], S2P[:, 1, 1, :], id2[:, :], ALU.add).then_inc(s2_done, 1)
            rstd_of(0, 0, var_done, rstd_done)
            with gp.Fori(1, NT // 2) as p:
                for u in range(2):
                    x_minus_1(p * 2 + u, u)
                    rstd_of(p * 2 + (u - 1), 1 - u, var_done, rstd_done)
            rstd_of(NT - 1, 1, var_done, rstd_done)
            with gp.Fori(0, NT // 2) as p:
                for u in range(2):
                    rstd_of(p * 2 + u, u, var2_done, rstd2_done)

        @block.tensor
        def _(pe):
            mm, tr = nc.tensor.matmul, nc.tensor.transpose
            pe.wait_ge(consts, 6)

            def x_transpose(t, u):
                pe.wait_ge(x_in[u], (t - u) * 8 + 16)
                for k in range(KC):
                    last = tr(pb[u][:, k * P:(k + 1) * P], xs[:, u, k * P:(k + 1) * P], idf[:, :])
                last.then_inc(xT_ps, 1)

            def seq_product(t, u, bank_used=True, bank4_used=True, wa=False):
                pe.wait_ge(xT_sb, t + 1)
                if bank_used:
                    pe.wait_ge(seq_sb, t - 1)
                for k in range(KC):
                    last = mm(pb[2 + u][:, :], xT[:, u, k * P:(k + 1) * P], WS[:, k, :], start=(k == 0), stop=(k == KC - 1))
                last.then_inc(seq_ps, 1)
                if wa:
                    pe.wait_ge(wa_done, 1)
                if bank4_used:
                    pe.wait_ge(s_sb, t)
                for k in range(KC):
                    last = mm(pb[4][:, 0:2 * H], xT[:, u, k * P:(k + 1) * P], WA[:, k, :], start=(k == 0), stop=(k == KC - 1))
                last.then_inc(s_ps, 1)

            def mask_tiles(t, u, banks_used=True):
                pe.wait_ge(mask_done, t + 1)
                for half, (ps, evacuated, bank) in enumerate(((mtA_ps, mtA_sb, 5), (mtB_ps, mtB_sb, 6))):
                    if banks_used:
                        pe.wait_ge(evacuated, t)
                    bk = pb[bank][:, :].bitcast(bf16)
                    for jj in range(HALF):
                        j = half * HALF + jj
                        last = tr(bk[:, jj * P:(jj + 1) * P], mask_b[:, u, j * P:(j + 1) * P], idb[:, :])
                    last.then_inc(ps, 1)

            x_transpose(0, 0)
            pe.wait_ge(wseq_in, 16)
            seq_product(0, 0, False, False, wa=True)
            x_transpose(1, 1)
            mask_tiles(0, 0, False)
            seq_product(1, 1, False)
            x_transpose(2, 0)
            mask_tiles(1, 1)
            with pe.Fori(1, NT // 2 - 1) as p:
                for u in range(2):
                    t = p * 2 + u
                    seq_product(t, u)
                    x_transpose(t + 1, 1 - u)
                    mask_tiles(t, u)
            seq_product(NT - 2, 0)
            x_transpose(NT - 1, 1)
            mask_tiles(NT - 2, 0)
            seq_product(NT - 1, 1)
            mask_tiles(NT - 1, 1)

            pe.wait_ge(s_sb, NT)
            pe.wait_ge(seq_sb, NT)
            for t in range(NT):
                last = tr(pb[t // 4][0:H, (t % 4) * P:(t % 4 + 1) * P], S1[:, :, t], idf[:, :])
                if t % 4 == 3:
                    last.then_inc(s1T_ps, 1)
            tr(pb[4][0:NT, 0:P], EMP[:, :], idf[:, :]).then_inc(ne_ps, 1)

            pe.wait_ge(tiles_added, NT)
            for j in range(NT):
                last = mm(pb[7][:, j:j + 1], CSA[:, j * P:(j + 1) * P], ones[:, 0:1], start=True, stop=True)
            last.then_inc(col_ps, 1)

            pe.wait_ge(s1T_sb, KC)
            pe.wait_ge(ne_sb, 1)
            pe.wait_ge(mtA_sb, NT)
            pe.wait_ge(mtB_sb, NT)
            pe.sem_inc(g_used, NG)

            with pe.Fori(0, H // 2) as p:
                for u in range(2):
                    h = p * 2 + u
                    pe.wait_ge(pn_ready, h + 1)
                    for j in range(NT):
                        s = (u * NT + j) % NG
                        pe.wait_ge(g_ready, h * NT + (j + 1))
                        for i in range(NT):
                            bank, c = i // IB, (i % IB) * 4 * DV
                            if j == 0 and i % IB == 0:
                                pe.wait_ge(bank_free, h * NB + (bank + 1))
                            mm(pb[bank][:, c:c + 4 * DV], G[:, s, i * P:(i + 1) * P],
                               PN[:, u, j, 0:4, :].rearrange("p c d -> p (c d)"),
                               start=(j == 0 and i % IB == 0), stop=(j == NT - 1), skip_group_check=True)
                            last = mm(pb[bank][:, c + 2 * DV:c + 4 * DV], MT[:, j, i * P:(i + 1) * P],
                                      PN[:, u, j, 4:6, :].rearrange("p c d -> p (c d)"),
                                      start=False, stop=(j == NT - 1), skip_group_check=True)
                        last.then_inc(g_used, 1)

            def general_products():
                pe.wait_ge(gen_seq_in, 16)
                with pe.Fori(0, H) as h:
                    pe.wait_ge(gen_diag, h + 1)
                    for k in range(4):
                        last = mm(pb[k][:, :], onesf, WT[:, k * 512:(k + 1) * 512], start=True, stop=True)
                    last.then_inc(gen_s2_ps, 1)
                    with pe.Fori(0, NT) as t:
                        pe.wait_ge(gen_exp, h * NT + t + 1)
                        for j in range(NT):
                            last = tr(pb[j // 4][:, (j % 4) * P:(j % 4 + 1) * P], SCO[:, j * P:(j + 1) * P], idf[:, :])
                        last.then_inc(gen_wt_ps, 1)
                        pe.wait_ge(gen_wt_sb, h * NT + t + 1)
                        for j in range(NT):
                            last = mm(pb[4][:, 0:DV], WT[:, j * P:(j + 1) * P],
                                      SEQ[:, j, DS(h, 1), :].rearrange("p o d -> p (o d)"), start=(j == 0), stop=(j == NT - 1))
                        last.then_inc(gen_res_ps, 1)
                pe.wait_ge(gen_head, H)

            pe.wait_ge(flag_ready, 1)
            with pe.If(pe.value_load(FLAG[0:1, 0:1], min_val=0, max_val=1) > 0):
                general_products()

            pe.wait_ge(hid_done, H)
            pe.wait_ge(wout_in, 16)

            def hid_transpose(t, u):
                for k in range(KC):
                    last = tr(pb[u][:, k * P:(k + 1) * P], HC[:, u, k * P:(k + 1) * P], idf[:, :])
                last.then_inc(hT_ps, 1)

            def out_product(t, u, bank_used=True):
                pe.wait_ge(hT_sb, t + 1)
                if bank_used:
                    pe.wait_ge(v_added, t - 1)
                for k in range(KC):
                    last = mm(pb[2 + u][:, :], hT[:, u, k * P:(k + 1) * P], WO[:, k, :], start=(k == 0), stop=(k == KC - 1))
                last.then_inc(o_ps, 1)

            def hid_wait(t):
                pe.wait_ge(hc_done, t + 1)

            for t in range(2):
                hid_wait(t)
                hid_transpose(t, t)
            out_product(0, 0, False)
            hid_wait(2)
            hid_transpose(2, 0)
            out_product(1, 1, False)
            with pe.Fori(1, NT // 2 - 1) as p:
                for u in range(2):
                    hid_wait(p * 2 + (u + 1))
                    hid_transpose(p * 2 + (u + 1), 1 - u)
                    out_product(p * 2 + u, u)
            hid_wait(NT - 1)
            hid_transpose(NT - 1, 1)
            out_product(NT - 2, 0)
            out_product(NT - 1, 1)

            def product(t, u, free, free_at, ready, moving, done, each=None):
                if free is not None:
                    pe.wait_ge(free, free_at)
                pe.wait_ge(ready, t + 1)
                for j in range(NT):
                    if each is not None:
                        pe.wait_ge(each, j + 1)
                    for l in range(2):
                        last = mm(pb[4 + 2 * u + l][:, :], S2P[:, u, j, :], moving[:, l, j, :],
                                  start=(j == 0), stop=(j == NT - 1))
                last.then_inc(done, 1)

            product(0, 0, bank_free, (H + 1) * NB, s2_done, XH, y_ps, each=xl_done)
            product(1, 1, None, 0, s2_done, XH, y_ps)
            with pe.Fori(1, NT // 2) as p:
                for u in range(2):
                    t = p * 2 + u
                    product(t, u, yv_done, t - 1, s2_done, XH, y_ps)
            product(0, 0, yv_done, NT - 1, pan_done, ZH, o2_ps, each=zl_done)
            product(1, 1, yv_done, NT, pan_done, ZH, o2_ps)
            with pe.Fori(1, NT // 2) as p:
                for u in range(2):
                    t = p * 2 + u
                    product(t, u, ov_done, t - 1, pan_done, ZH, o2_ps)

        @block.scalar
        def _(sc):
            A = nc.scalar.activation

            def cast_adj(t, u, fresh=False):
                sc.wait_ge(adj_in[u], (t - u) * 8 + 16)
                if not fresh:
                    sc.wait_ge(tiles_added, t - 1)
                    sc.wait_ge(mask_done, t - 1)
                A(adj_b[:, u, :], adj_f[:, u, :], ACT.Copy, accum_out=RS[:, u:u + 1]).then_inc(adjb_done, 1)

            def evacuate(t, u):
                sc.wait_ge(seq_ps, t + 1)
                A(SEQ[:, DS(t, 1), :, 0:DH].rearrange("p o h d -> p (o h) d"),
                  pb[2 + u][:, :].rearrange("p (h d) -> p h d", d=DH), ACT.Copy).then_inc(seq_sb, 1)
                sc.wait_ge(mtA_ps, t + 1)
                A(MT[:, 0:HALF, DS(t * P, P)],
                  pb[5][:, :].bitcast(bf16).rearrange("p (j i) -> p j i", i=P), ACT.Copy).then_inc(mtA_sb, 1)

            cast_adj(0, 0, True)
            cast_adj(1, 1, True)
            evacuate(0, 0)
            with sc.Fori(1, NT // 2) as p:
                for u in range(2):
                    cast_adj(p * 2 + u, u)
                    evacuate(p * 2 + (u - 1), 1 - u)
            evacuate(NT - 1, 1)

            for k in range(KC):
                sc.wait_ge(s1T_ps, k + 1)
                A(s1T[:, k * 512:(k + 1) * 512], pb[k][0:H, :], ACT.Copy, scale=-BIG).then_inc(s1T_sb, 1)
            sc.wait_ge(texp_in, 1)
            A(FF, EE, ACT.Exp, scale=SLOPE).then_inc(act, 1)
            A(AA, AA, ACT.Exp, scale=1.0 - SLOPE).then_inc(act, 1)
            A(BBT, BBT, ACT.Exp, scale=SLOPE - 1.0).then_inc(act, 1)
            sc.wait_ge(act, 3)
            A(EE, EE, ACT.Exp).then_inc(texp_out, 1)

            def low_sums(h, first=False):
                sc.wait_ge(g_used, h * NT + (NT + NG))
                if not first:
                    sc.wait_ge(comb_ready, h)
                for b in range(NB):
                    n = min(IB, NT - b * IB)
                    A(T[:, b * IB:b * IB + n, :, :], sums(b, n)[:, :, :, 1, :], ACT.Copy, scale=UNSPLIT).then_inc(lo_out, 1)

            def high_operands(h, u):
                sc.wait_ge(v2_ready, h * 2 + 2)
                A(PN[:, u, :, 0:5:4, :], V2[:, :, :, :], ACT.Copy, scale=UNSPLIT).then_inc(hi_ready, 1)

            def att_head(h, u, lows=2, first=False, last=False):
                sc.wait_ge(s1b_in[u], (h - u) * 8 + 16)
                sc.wait_ge(kb_ready, h + 1)
                for j in range(NT):
                    if j in ACTZ:
                        n = ACTZ.index(j)
                        if n >= NZ:
                            sc.wait_ge(g_ready, h * NT + (ACTZ[n - NZ] + 1))
                        elif not first:
                            sc.wait_ge(g_ready, h * NT + (ACTZ[n - NZ] + 1 - NT))
                        A(Z[:, (u * NV + n) % NZ, :], S1B[:, u, :], ACT.Relu, bias=KB[:, u, j:j + 1], scale=-1.0).then_inc(z_ready, 1)
                    if j == SHARED:
                        if not first:
                            sc.wait_ge(g_ready, h * NT)
                        A(ZS1[:, :], S1B[:, u, 0:SC], ACT.Relu, bias=KB[:, u, j:j + 1], scale=-1.0).then_inc(zs_ready, 1)
                    if j == AT_SUMS and lows:
                        low_sums(h - 1, first=(lows == 1))
                    if j == AT_HIGH and not last:
                        high_operands(h + 1, 1 - u)

            sc.wait_ge(mtA_ps, NT)
            sc.wait_ge(mtB_ps, NT)
            sc.wait_ge(col_ps, 1)
            high_operands(0, 0)
            att_head(0, 0, lows=0, first=True)
            att_head(1, 1, lows=1)
            with sc.Fori(1, H // 2 - 1) as p:
                for u in range(2):
                    att_head(p * 2 + u, u)
            att_head(H - 2, 0)
            att_head(H - 1, 1, last=True)
            low_sums(H - 1)

            def move_hT(t, u, fresh=False):
                sc.wait_ge(hT_ps, t + 1)
                if not fresh:
                    sc.wait_ge(o_ps, t - 1)
                A(hT[:, u, :], pb[u][:, :], ACT.Copy).then_inc(hT_sb, 1)

            def copy_hid(t, u, fresh=False):
                if not fresh:
                    sc.wait_ge(hT_ps, t - 1)
                A(HC[:, u, :].rearrange("p (h d) -> p h d", d=DH),
                  SEQ[:, DS(t, 1), :, 0:DH].rearrange("p o h d -> p (o h) d"), ACT.Copy).then_inc(hc_done, 1)

            def elu_exp(t, u):
                sc.wait_ge(v_added, t + 1)
                A(ee[:, u, :], vv[:, u, :], ACT.Exp).then_inc(ex_done, 1)

            def scale_x(t, u, fresh=False):
                sc.wait_ge(x1_done, t + 1)
                if not fresh:
                    sc.wait_ge(xl_done, t - 1)
                A(v2x[:, u, :], X1[:, DS(t, 1), 0:D].rearrange("p o d -> p (o d)"), ACT.Copy,
                  scale=DSX[:, DS(t, 1)]).then_inc(v2x_done, 1)

            def high_x(t, u):
                sc.wait_ge(v2x_done, t + 1)
                A(XH[:, 0, DS(t, 1), :].rearrange("p o d -> p (o d)"), v2x[:, u, :], ACT.Copy, scale=UNSPLIT).then_inc(xh_done, 1)

            def general_exponentials():
                with sc.Fori(0, H) as h:
                    sc.wait_ge(gen_s2_ps, h + 1)
                    for k in range(4):
                        A(S2B[:, k * 512:(k + 1) * 512], pb[k][:, :], ACT.Copy).then_inc(gen_s2_sb, 1)
                    with sc.Fori(0, NT) as t:
                        sc.wait_ge(gen_max, h * NT + t + 1)
                        A(SCO, SCO, ACT.Exp, bias=NEGM).then_inc(gen_exp, 1)
                        sc.wait_ge(gen_wt_ps, h * NT + t + 1)
                        for k in range(3):
                            A(WT[:, k * 512:(k + 1) * 512], pb[k][:, :], ACT.Copy)
                        A(WT[:, 3 * 512:4 * 512], pb[3][:, :], ACT.Copy).then_inc(gen_wt_sb, 1)
                sc.wait_ge(gen_head, H)

            sc.wait_ge(g_ready, H * NT)
            sc.wait_ge(flag_ready, 1)
            with sc.If(sc.value_load(FLAG[0:1, 0:1], min_val=0, max_val=1) > 0):
                general_exponentials()
            sc.wait_ge(hid_done, H)
            sc.wait_ge(g_used, H * NT + NG)
            copy_hid(0, 0, True)
            copy_hid(1, 1, True)
            move_hT(0, 0, True)
            copy_hid(2, 0)
            move_hT(1, 1, True)

            def first_layer(t, u, n=None):
                if n is None or n < NT - 1:
                    move_hT(t + 1, 1 - u)
                if n is None or n < NT - 2:
                    copy_hid(t + 2, u)
                if n is None or n <= NT:
                    elu_exp(t - 1, 1 - u)
                if n is None or n >= 3:
                    scale_x(t - 3, 1 - u, n is not None and n < 5)
                    high_x(t - 3, 1 - u)

            for t in range(1, 6):
                first_layer(t, t % 2, t)
            with sc.Fori(3, NT // 2 - 1) as p:
                for u in range(2):
                    first_layer(p * 2 + u, u)
            for t in range(NT - 2, NT + 3):
                first_layer(t, t % 2, t)

            def low_y(t, u, fresh=False):
                sc.wait_ge(y_ps, t + 1)
                if not fresh:
                    sc.wait_ge(yv_done, t - 1)
                A(lw[:, u, :], pb[5 + 2 * u][:, :], ACT.Copy, scale=DSL[:, DS(t, 1)]).then_inc(yl_done, 1)

            def high_z(t, u):
                sc.wait_ge(yv_done, t + 1)
                A(ZH[:, 0, DS(t, 1), :].rearrange("p o d -> p (o d)"), yw[:, u, :], ACT.Copy, scale=UNSPLIT).then_inc(zh_done, 1)

            sc.wait_ge(xl_done, NT)
            for u in range(2):
                low_y(u, u, True)
                high_z(u, u)
            with sc.Fori(1, NT // 2) as p:
                for u in range(2):
                    low_y(p * 2 + u, u)
                    high_z(p * 2 + u, u)

            def low_o(t, u, free, free_at):
                sc.wait_ge(o2_ps, t + 1)
                sc.wait_ge(free, free_at)
                A(lw[:, u, :], pb[5 + 2 * u][:, :], ACT.Copy, scale=UNSPLIT / ZS).then_inc(ol_done, 1)

            for u in range(2):
                low_o(u, u, yv_done, NT)
            with sc.Fori(1, NT // 2) as p:
                for u in range(2):
                    low_o(p * 2 + u, u, ov_done, p * 2 + (u - 1))

        @block.vector
        def _(ve):
            V = nc.vector
            own = Steps(dve)
            ve.wait_ge(wseq_in, 16)
            ve.wait_ge(a_in, 32)
            ws_v = WS.rearrange("p k (h d) -> p (k h) d", d=DH)
            for i in range(2):
                own.mark(V.tensor_tensor(WAtmp, ws_v, AV[:, i, :].unsqueeze(1).broadcast_to([P, KC * H, DH]), ALU.mult))
                own.wait(ve)
                own.mark(V.tensor_reduce(WA[:, :, i * H:(i + 1) * H], WAtmp, AX.X, ALU.add))
                own.wait(ve)
            V.memset(KB[:, :, :], 0.0).then_inc(wa_done, 1)

            def move_xT(t, u, fresh=False):
                ve.wait_ge(xT_ps, t + 1)
                if not fresh:
                    ve.wait_ge(s_ps, t - 1)
                V.tensor_copy(xT[:, u, :], pb[u][:, :]).then_inc(xT_sb, 1)

            def prologue_tile(t, u, fresh=False, more=True, more_fresh=False):
                ve.wait_ge(adjb_done, t + 1)
                own.mark(V.tensor_scalar(EMP[:, DS(t, 1)], RS[:, u:u + 1], 0.0, None, ALU.is_equal))
                V.tensor_copy(ROW[:, DS(t, 1)], RS[:, u:u + 1]).then_inc(row_done, 1)
                own.wait(ve)
                if not fresh:
                    ve.wait_ge(mtB_ps, t - 1)
                V.tensor_scalar(mask_b[:, u, :], adj_b[:, u, :], EMP[:, DS(t, 1)], None, ALU.max).then_inc(mask_done, 1)
                if not fresh or u:
                    ve.wait_ge(tiles_added, t)
                V.tensor_tensor(CSA, CSA, adj_b[:, u, :], ALU.add).then_inc(tiles_added, 1)
                ve.wait_ge(s_ps, t + 1)
                V.tensor_copy(TAB[:, 0:2, :, DS(t, 1)].rearrange("p e h o -> p e (h o)"),
                              pb[4][:, 0:2 * H].rearrange("p (e h) -> p e h", e=2)).then_inc(s_sb, 1)
                if more:
                    move_xT(t + 1, 1 - u, more_fresh)
                ve.wait_ge(seq_sb, t + 1)
                V.tensor_reduce(VMT[:, DS(t, 1), :].rearrange("p o h -> p (o h)"),
                                SEQ[:, DS(t, 1), :, 0:DH].rearrange("p o h d -> p (o h) d"), AX.X, ALU.max,
                                apply_absolute_value=True).then_inc(vm_done, 1)
                ve.wait_ge(mtB_ps, t + 1)
                V.tensor_copy(MT[:, HALF:NT, DS(t * P, P)],
                              pb[6][:, :].bitcast(bf16).rearrange("p (j i) -> p j i", i=P)).then_inc(mtB_sb, 1)

            ve.wait_ge(consts, 6)
            move_xT(0, 0, True)
            prologue_tile(0, 0, fresh=True, more_fresh=True)
            prologue_tile(1, 1, fresh=True)
            with ve.Fori(1, NT // 2 - 1) as p:
                own.enter(p, 1, 2)
                for u in range(2):
                    prologue_tile(p * 2 + u, u)
                own.leave(NT // 2 - 1)
            prologue_tile(NT - 2, 0)
            prologue_tile(NT - 1, 1, more=False)

            ve.wait_ge(vm_done, NT)
            V.tensor_reduce(red[:, 0, :], VMT.rearrange("p t h -> p h t"), AX.X, ALU.max).then_inc(red_done, 1)
            ve.wait_ge(s_sb, NT)
            V.tensor_reduce(red[:, 1, :], S2, AX.X, ALU.max).then_inc(red_done, 1)
            ve.wait_ge(ne_ps, 1)
            V.tensor_scalar(NEr[:, :], pb[4][0:NT, 0:P], -1.0, 1.0, ALU.mult, ALU.add).then_inc(ne_sb, 1)
            ve.wait_ge(allred, 1)
            c2b = C2[:, :].unsqueeze(2).broadcast_to([P, H, NT])
            own.mark(V.tensor_scalar(VM[:, :], VM[:, :], 1e-30, None, ALU.max))
            own.mark(V.tensor_tensor(EE, S2, c2b, ALU.subtract))
            own.mark(V.tensor_tensor(AA, S1, c2b, ALU.add))
            own.wait(ve)
            own.mark(V.tensor_scalar(BBT, AA, 0.0, None, ALU.max))
            own.wait(ve)
            own.mark(V.tensor_scalar(AA, AA, 0.0, None, ALU.min))
            own.wait(ve)
            V.tensor_scalar(S2, S2, BIG, None, ALU.mult).then_inc(texp_in, 1)
            own.mark(V.tensor_copy(SEQ[:, :, :, DH], VM[:, :].unsqueeze(1).broadcast_to([P, NT, H])))
            own.mark(V.reciprocal(RV[:, :], VM[:, :]))
            own.wait(ve)
            own.mark(V.tensor_scalar(RV[:, :], RV[:, :], TOP * SPLIT, None, ALU.mult))
            own.wait(ve)
            rvb = RV[:, :].unsqueeze(2).broadcast_to([P, H, NT])
            ve.wait_ge(texp_out, 1)
            own.mark(V.tensor_tensor(EE, EE, rvb, ALU.mult))
            own.mark(V.tensor_tensor(FF, FF, rvb, ALU.mult))
            own.wait(ve)
            V.memset(RD[:, :], 1.0).then_inc(tabs_done, 1)

            def low_operands(h, u):
                ve.wait_ge(hi_ready, h + 1)
                own.mark(V.scalar_tensor_tensor(PN[:, u, :, 1, :], PN[:, u, :, 0, :], -SPLIT, V2[:, :, 0, :], ALU.mult, ALU.add))
                own.mark(V.scalar_tensor_tensor(PN[:, u, :, 5, :], PN[:, u, :, 4, :], -SPLIT, V2[:, :, 1, :], ALU.mult, ALU.add))
                own.wait(ve)
                V.tensor_scalar(PN[:, u, :, 2:4, :].rearrange("p t c d -> p t (c d)"),
                                PN[:, u, :, 4:6, :].rearrange("p t c d -> p t (c d)"), -1.0, None, ALU.mult).then_inc(pn_ready, 1)

            def high_sums(h):
                for b in range(NB):
                    n = min(IB, NT - b * IB)
                    ve.wait_ge(lo_out, h * NB + (b + 1))
                    V.tensor_tensor(T[:, b * IB:b * IB + n, :, :], sums(b, n)[:, :, :, 0, :], T[:, b * IB:b * IB + n, :, :],
                                    ALU.add).then_inc(bank_free, 1)

            def hidden_head(h):
                ve.wait_ge(comb_ready, h + 1)
                own.mark(V.reciprocal(RD[:, :], ND[:, :, DH]))
                own.wait(ve)
                V.scalar_tensor_tensor(SEQ[:, :, DS(h, 1), 0:DH].rearrange("p t o d -> p t (o d)"), ND[:, :, 0:DH],
                                       VM[:, DS(h, 1)], RD[:, :].unsqueeze(2).broadcast_to([P, NT, DH]),
                                       ALU.mult, ALU.mult).then_inc(hid_done, 1)

            def att_head(h, u, first=False, last=False):
                ve.wait_ge(s1b_in[u], (h - u) * 8 + 16)
                ve.wait_ge(kb_ready, h + 1)
                for j in range(NT):
                    s = (u * NT + j) % NG
                    ve.wait_ge(g_used, h * NT + (j + 1))
                    if j in ACTZ:
                        n = ACTZ.index(j)
                        ve.wait_ge(z_ready, h * NV + (n + 1))
                        V.tensor_tensor(G[:, s, :], Z[:, (u * NV + n) % NZ, :], MT[:, j, :], ALU.min).then_inc(g_ready, 1)
                    elif j == SHARED:
                        V.scalar_tensor_tensor(G[:, s, SC:N], S1B[:, u, SC:N], KB[:, u, j:j + 1], MT[:, j, SC:N],
                                               ALU.is_lt, ALU.mult)
                        ve.wait_ge(zs_ready, h + 1)
                        V.tensor_tensor(G[:, s, 0:SC], ZS1[:, :], MT[:, j, 0:SC], ALU.min).then_inc(g_ready, 1)
                    else:
                        V.scalar_tensor_tensor(G[:, s, :], S1B[:, u, :], KB[:, u, j:j + 1], MT[:, j, :],
                                               ALU.is_lt, ALU.mult).then_inc(g_ready, 1)
                    if j == AT_SUMS and not first:
                        high_sums(h - 1)
                    if j == AT_LOW and not last:
                        low_operands(h + 1, 1 - u)
                    if j == AT_HID and not first:
                        hidden_head(h - 1)

            ve.wait_ge(adjb_done, NT)
            low_operands(0, 0)
            ve.sem_inc(bank_free, NB)
            att_head(0, 0, first=True)
            ve.wait_ge(col_ps, 1)
            ve.wait_ge(row_done, NT)
            own.mark(V.tensor_tensor(ROW[:, :], pb[7][:, 0:NT], ROW[:, :], ALU.add))
            own.wait(ve)
            own.mark(V.tensor_scalar(ROW[:, :], ROW[:, :], 0.5, 1.0, ALU.mult, ALU.add))
            own.wait(ve)
            V.tensor_scalar(DINV[:, :], ROW[:, :], 1e-30, None, ALU.max).then_inc(deg_done, 1)
            ve.wait_ge(seq_stored, 16)
            att_head(1, 1)
            own.mark(V.tensor_reduce(RV[:, :], S2, AX.X, ALU.min))
            own.wait(ve)
            own.mark(V.scalar_tensor_tensor(RV[:, :], RV[:, :], 1.0 / BIG, C2[:, :], ALU.mult, ALU.subtract))
            own.wait(ve)
            own.mark(V.tensor_reduce(WID[:, 0:1], RV[:, :], AX.X, ALU.min))
            own.wait(ve)
            own.mark(V.tensor_scalar(WID[:, 1:2], WID[:, 0:1], -SPREAD, None, ALU.is_ge))
            own.wait(ve)
            V.tensor_scalar(WID[:, 2:3], WID[:, 1:2], -1.0, 1.0, ALU.mult, ALU.add).then_inc(spread_done, 1)
            ve.wait_ge(pow_done, 1)
            own.mark(V.scalar_tensor_tensor(DINV[:, :], ROW[:, :], 0.0, DINV[:, :], ALU.is_gt, ALU.mult))
            own.wait(ve)
            V.tensor_scalar(DSX[:, :], DINV[:, :], XS * SPLIT, None, ALU.mult).then_inc(dscale, 1)
            V.tensor_scalar(DSZ[:, :], DINV[:, :], 0.5 / XS * ZS * SPLIT, None, ALU.mult).then_inc(dscale, 1)
            V.tensor_scalar(DSL[:, :], DINV[:, :], 0.5 / XS * ZS, None, ALU.mult).then_inc(dscale, 1)
            ve.wait_ge(dscale, 3)
            with ve.Fori(1, H // 2 - 1) as p:
                own.enter(p, 1, 6)
                for u in range(2):
                    att_head(p * 2 + u, u)
                own.leave(H // 2 - 1)
            att_head(H - 2, 0)
            att_head(H - 1, 1, last=True)
            high_sums(H - 1)
            ve.wait_ge(bank_free, H * NB + NB)
            ve.wait_ge(comb_ready, H - 1)
            for e, tab in enumerate((AA, BBT)):
                own.mark(V.tensor_tensor(T[:, :, e, :], T[:, :, e, :], tab[:, H - 1, :].unsqueeze(2).broadcast_to([P, NT, DV]), ALU.mult))
            own.wait(ve)
            V.tensor_tensor(ND[:, :, :], T[:, :, 0, :], T[:, :, 1, :], ALU.add).then_inc(comb_ready, 1)
            hidden_head(H - 1)

            def general_scores():
                ve.wait_ge(g_used, H * NT + NG)
                V.memset(onesf, 1.0).then_inc(gen_scores, 1)
                with ve.Fori(0, H) as h:
                    own_h = lambda s: s[:, DS(h, 1), :].rearrange("p o t -> p (o t)")
                    V.tensor_scalar(S2C, own_h(S2), 1.0 / BIG, None, ALU.mult).then_inc(gen_rcp, 1)
                    ve.wait_ge(gen_rcp, h * 2 + 1)
                    V.tensor_tensor(WT.rearrange("p (t i) -> p t i", t=NT), idf[:, :].unsqueeze(1).broadcast_to([P, NT, P]),
                                    S2C.unsqueeze(2).broadcast_to([P, NT, P]), ALU.mult).then_inc(gen_diag, 1)
                    ve.wait_ge(gen_s2_sb, h * 4 + 4)
                    V.memset(NEGM, 0.0)
                    with ve.Fori(0, NT) as t:
                        s1 = S1[:, DS(h, 1), DS(t, 1)].rearrange("p o t -> p (o t)")
                        V.tensor_scalar(SCO, S2B, s1, None, ALU.add).then_inc(gen_sum, 1)
                        ve.wait_ge(gen_adj_in, h * (16 * NT) + t * 16 + 16)
                        V.tensor_scalar(ADJ, ADJ, 1.0, -MASKED, ALU.subtract, ALU.mult).then_inc(gen_sum, 1)
                        ve.wait_ge(gen_sum, h * (2 * NT) + t * 2 + 2)
                        V.scalar_tensor_tensor(SCO, SCO, SLOPE, SCO, ALU.mult, ALU.max).then_inc(gen_leaky, 1)
                        ve.wait_ge(gen_leaky, h * NT + t + 1)
                        V.tensor_tensor(SCO, SCO, ADJ, ALU.add).then_inc(gen_scores, 1)
                        ve.wait_ge(gen_scores, h * NT + t + 2)
                        V.tensor_reduce(NEGM, SCO, AX.X, ALU.max, negate=True).then_inc(gen_max, 1)
                        ve.wait_ge(gen_res_ps, h * NT + t + 1)
                        V.tensor_copy(RES[:, DS(t, 1), :].rearrange("p o d -> p (o d)"), pb[4][:, 0:DV]).then_inc(gen_res, 1)
                    ve.wait_ge(gen_res, h * NT + NT)
                    V.reciprocal(RD[:, :], RES[:, :, DH]).then_inc(gen_rcp, 1)
                    ve.wait_ge(gen_rcp, h * 2 + 2)
                    V.scalar_tensor_tensor(SEQ[:, :, DS(h, 1), 0:DH].rearrange("p t o d -> p t (o d)"), RES[:, :, 0:DH],
                                           VM[:, DS(h, 1)], RD[:, :].unsqueeze(2).broadcast_to([P, NT, DH]),
                                           ALU.mult, ALU.mult).then_inc(gen_head, 1)
                ve.wait_ge(gen_head, H)

            ve.wait_ge(flag_ready, 1)
            with ve.If(ve.value_load(FLAG[0:1, 0:1], min_val=0, max_val=1) > 0):
                general_scores()

            def restore_and_add(t, u, fresh=False):
                mt = MT[:, :, DS(t * P, P)]
                own.mark(V.tensor_tensor(mt, mt, NEB[:, DS(t * P, P)].unsqueeze(1).broadcast_to([P, NT, P]), ALU.mult))
                own.wait(ve)
                ve.wait_ge(ap_in[u], (t - u) * 8 + 16)
                if not fresh:
                    ve.wait_ge(y_ps, t - 1)
                own.mark(V.tensor_tensor(S2P[:, u, :, :], APN[:, u, :, :], mt, ALU.add))
                own.wait(ve)
                diag = S2P[:, u, DS(t, 1), :].rearrange("p o i -> p (o i)")
                V.tensor_tensor(diag, diag, id2[:, :], ALU.add).then_inc(s2_done, 1)

            ve.wait_ge(ne_in, 16)
            restore_and_add(0, 0, True)

            ve.wait_ge(bb_in, 16)

            def norm_stats(src, u, done, between):
                own.mark(V.bn_stats(bst[:, u, :], src))
                own.wait(ve)
                between()
                own.mark(V.bn_aggr(mv[:, u, :], bst[:, u, :]))
                own.wait(ve)
                V.tensor_scalar(vps[:, u:u + 1], mv[:, u, 1:2], EPS, None, ALU.add).then_inc(done, 1)

            def add_bias(t, u):
                ve.wait_ge(o_ps, t + 1)
                V.tensor_tensor(vv[:, u, :], pb[2 + u][:, :], BB, ALU.add).then_inc(v_added, 1)

            def low_x(t, u):
                ve.wait_ge(xh_done, t + 1)
                xt = lambda l: XH[:, l, DS(t, 1), :].rearrange("p o d -> p (o d)")
                V.scalar_tensor_tensor(xt(1), xt(0), -SPLIT, v2x[:, u, :], ALU.mult, ALU.add).then_inc(xl_done, 1)

            def first_layer(t, u, n=None):
                elu = n is None or 1 <= n <= NT
                norm = n is None or 2 <= n < NT + 2
                v = 1 - u
                if elu:
                    ve.wait_ge(v_added, t)
                    ve.wait_ge(xm_done, t)
                    V.scalar_tensor_tensor(rr[:, v, :], vv[:, v, :], 0.0, xr[:, v, :], ALU.max, ALU.add).then_inc(xr_used, 1)
                if n is None or n < NT:
                    add_bias(t, u)
                if elu:
                    ve.wait_ge(xr_used, t)
                    ve.wait_ge(ex_done, t)
                    own.mark(V.scalar_tensor_tensor(rr[:, v, :], ee[:, v, :], 1.0, rr[:, v, :], ALU.min, ALU.add))
                if n is None or 4 <= n:
                    low_x(t - 4, u)
                if elu:
                    own.wait(ve)
                    own.mark(V.bn_stats(bst[:, v, :], rr[:, v, :]))
                if norm:
                    x1 = X1[:, DS(t - 2, 1), 0:D].rearrange("p o d -> p (o d)")
                    ve.wait_ge(rstd_done, t - 1)
                    ve.wait_ge(hc_done, t - 1)
                if elu:
                    own.wait(ve)
                if norm:
                    V.tensor_scalar(x1, rr[:, u, :], mv[:, u, 0:1], rstd[:, u:u + 1], ALU.subtract, ALU.mult).then_inc(x1_done, 1)
                if elu:
                    own.mark(V.bn_aggr(mv[:, v, :], bst[:, v, :]))
                    own.wait(ve)
                    V.tensor_scalar(vps[:, v:v + 1], mv[:, v, 1:2], EPS, None, ALU.add).then_inc(var_done, 1)

            for t in range(4):
                first_layer(t, t % 2, t)
            with ve.Fori(2, NT // 2) as p:
                own.enter(p, 2, 6)
                for u in range(2):
                    first_layer(p * 2 + u, u)
                own.leave(NT // 2)
            for t in range(NT, NT + 4):
                first_layer(t, t % 2, t)

            def z_sum(t, u, fresh=False):
                ve.wait_ge(yl_done, t + 1)
                if not fresh:
                    ve.wait_ge(zl_done, t - 1)
                V.scalar_tensor_tensor(yw[:, u, :], pb[4 + 2 * u][:, :], DSZ[:, DS(t, 1)], lw[:, u, :],
                                       ALU.mult, ALU.add).then_inc(yv_done, 1)

            def low_z(t, u):
                ve.wait_ge(zh_done, t + 1)
                zt = lambda l: ZH[:, l, DS(t, 1), :].rearrange("p o d -> p (o d)")
                V.scalar_tensor_tensor(zt(1), zt(0), -SPLIT, yw[:, u, :], ALU.mult, ALU.add).then_inc(zl_done, 1)

            def copy_panel(t, u, free, free_at):
                ve.wait_ge(free, free_at)
                V.tensor_copy(S2P[:, u, :, :], MT[:, :, DS(t * P, P)]).then_inc(pan_done, 1)

            for t in range(2):
                z_sum(t, t, True)
                low_z(t, t)
                restore_and_add(t + 2, t)
            with ve.Fori(1, NT // 2 - 1) as p:
                own.enter(p, 1, 4)
                for u in range(2):
                    t = p * 2 + u
                    z_sum(t, u)
                    low_z(t, u)
                    restore_and_add(t + 2, u)
                own.leave(NT // 2 - 1)
            z_sum(NT - 2, 0)
            low_z(NT - 2, 0)
            copy_panel(0, 0, y_ps, NT - 1)
            z_sum(NT - 1, 1)
            low_z(NT - 1, 1)
            copy_panel(1, 1, y_ps, NT)

            def o_sum(t, u, between, fresh=False):
                ve.wait_ge(ol_done, t + 1)
                if not fresh:
                    ve.wait_ge(out_st[u], (t - u) * 8)
                own.mark(V.scalar_tensor_tensor(yw[:, u, :], pb[4 + 2 * u][:, :], 1.0 / ZS, lw[:, u, :], ALU.mult, ALU.add))
                own.wait(ve)
                V.tensor_tensor(yw[:, u, :], yw[:, u, :], X1[:, DS(t, 1), 0:D].rearrange("p o d -> p (o d)"), ALU.add).then_inc(ov_done, 1)
                ve.wait_ge(ov_done, t + 1)
                norm_stats(yw[:, u, :], u, var2_done, between)

            def o_norm(t, u):
                ve.wait_ge(rstd2_done, t + 1)
                V.tensor_scalar(yw[:, u, :], yw[:, u, :], mv[:, u, 0:1], rstd[:, u:u + 1], ALU.subtract, ALU.mult).then_inc(out_ready, 1)

            for t in range(2):
                o_sum(t, t, lambda: copy_panel(t + 2, t, o2_ps, t + 1), True)
                o_norm(t, t)
            with ve.Fori(1, NT // 2 - 1) as p:
                own.enter(p, 1, 6)
                for u in range(2):
                    t = p * 2 + u
                    o_sum(t, u, lambda: copy_panel(t + 2, u, o2_ps, t + 1))
                    o_norm(t, u)
                own.leave(NT // 2 - 1)
            for t in (NT - 2, NT - 1):
                o_sum(t, t % 2, lambda: None)
                o_norm(t, t % 2)


_INS = ['x', 'adj', 'L0_gnn_W_seq', 'L0_gnn_a1', 'L0_gnn_a2', 'L0_gnn_W_out', 'L0_gnn_b_out']
_OUTS = [((2048, 512), 'float32')]


def kernel(**inputs):
    import numpy as _np
    import concourse.bacc as _bacc
    from concourse import mybir as _mybir
    from concourse.bass_utils import run_bass_kernel_spmd as _run

    nc = _bacc.Bacc("TRN2", target_bir_lowering=False, num_devices=1)
    arrays, args = {}, []
    for name in _INS:
        a = _np.ascontiguousarray(inputs[name])
        arrays[f"in_{name}_dram"] = a
        args.append(nc.dram_tensor(f"in_{name}_dram", a.shape, _mybir.dt.from_np(a.dtype), kind="ExternalInput").ap())
    for i, (shape, dtype) in enumerate(_OUTS):
        dt = _mybir.dt.from_np(_np.dtype(dtype))
        args.append(nc.dram_tensor(f"out_{i}_dram", shape, dt, kind="ExternalOutput").ap())
    args.append(nc.dram_tensor("s1_rows_dram", (16, 2048), _mybir.dt.float32, kind="Internal").ap())
    args.append(nc.dram_tensor("nonempty_dram", (2048,), _mybir.dt.bfloat16, kind="Internal").ap())
    args.append(nc.dram_tensor("seq_copy_dram", (128, 16 * 16 * 33), _mybir.dt.float32, kind="Internal").ap())
    gat_then_normalised_adjacency(nc, *args)
    r = _run(nc, [arrays], core_ids=[0])
    return r.results[0]["out_0_dram"]
```
